# Optimizing a Trainium2 kernel written in Bass

```python
import numpy as np
import jax
import jax.numpy as jnp

def _softmax(x, axis=-1):
    return jax.nn.softmax(x, axis=axis)

def _gelu(x):
    return jax.nn.gelu(x, approximate=True)

def _silu(x):
    return jax.nn.silu(x)

def _sigmoid(x):
    return jax.nn.sigmoid(x)

def _layernorm(x, axis=-1, eps=1e-05):
    m = jnp.mean(x, axis=axis, keepdims=True)
    v = jnp.var(x, axis=axis, keepdims=True)
    return (x - m) / jnp.sqrt(v + eps)

def _scatter_add(tgt, idx, src, axis=0):
    return tgt.at[idx].add(src)

def _segment_sum(src, seg, n):
    return jax.ops.segment_sum(src, seg, n)
kernel_name = 'mk_gnn_preln_d4_gnn_r32_002caf'

def setup_inputs(seed: int=0):
    np.random.seed(seed)
    _w = jnp.asarray

    def _rec_inputs():
        import jax
        import jax.numpy as jnp
        _gk = jax.random.key(seed)
        x = -0.000202 + 1 * jax.random.normal(jax.random.fold_in(_gk, 1), (3125, 128), jnp.float32)
        src = jax.random.randint(jax.random.fold_in(_gk, 2), (100000,), 0, 3125, jnp.int32)
        dst = jnp.minimum((3125 * jax.random.uniform(jax.random.fold_in(_gk, 3), (100000,)) ** 2.0).astype(jnp.int32), 99999)
        _o = jnp.argsort(dst, stable=True)
        src = src[_o]
        dst = dst[_o]
        edge_attr_16 = 0.000312547 + 1.00004 * jax.random.normal(jax.random.fold_in(_gk, 12), (100000, 16), jnp.float32)
        edge_type_1000 = jax.random.randint(jax.random.fold_in(_gk, 14), (100000,), 0, 1000, jnp.int32)
        edge_weight = jax.random.uniform(jax.random.fold_in(_gk, 15), (100000,), jnp.float32, 0.0, 0.999999)
        return (x, src, dst, edge_attr_16, edge_type_1000, edge_weight)
    x, src, dst, edge_attr_16, edge_type_1000, edge_weight = _rec_inputs()

    def _L0_gnn_setup():
        import jax, jax.numpy as jnp
        import numpy as np
        N_NODES = 50000
        N_EDGES = 25000
        D_FEAT = 128
        UNITS = 128

        def _degree(idx, n_nodes):
            deg = jnp.zeros((n_nodes,), dtype=jnp.float32).at[idx].add(1.0)
            return jnp.maximum(deg, 1.0)
        key = jax.random.key(seed)
        k1, k2, k3, k4 = jax.random.split(key, 4)
        x = jax.random.normal(k1, (N_NODES, D_FEAT), dtype=jnp.float32)
        source = jax.random.randint(k2, (N_EDGES,), 0, N_NODES, dtype=jnp.int32)
        target = jax.random.randint(k3, (N_EDGES,), 0, N_NODES, dtype=jnp.int32)
        W = jax.random.normal(k4, (D_FEAT, UNITS), dtype=jnp.float32) * (1.0 / np.sqrt(D_FEAT))
        b = jnp.zeros((UNITS,), dtype=jnp.float32)
        return {'x': x, 'source': source, 'target': target, 'W': W, 'b': b}
    _L0_gnn_all = _L0_gnn_setup()
    _L0_gnn_in = {k: v for k, v in _L0_gnn_all.items() if k in ('W', 'b')}
    del _L0_gnn_all

    def _L1_gnn_setup():
        import jax, jax.numpy as jnp
        import numpy as np
        N = 3125
        E = 50000
        D = 128
        L = 2
        key = jax.random.key(seed)
        k0, k1, k2, k3, k4 = jax.random.split(key, 5)
        x = jax.random.normal(k0, (N, D), dtype=jnp.float32)
        edge_index = jax.random.randint(k1, (2, E), 0, N, dtype=jnp.int32)
        edge_weight = jax.random.uniform(k2, (E,), dtype=jnp.float32)
        scale = 1.0 / np.sqrt(D)
        W_self = jax.random.normal(k3, (L, D, D), dtype=jnp.float32) * scale
        W_neigh = jax.random.normal(k4, (L, D, D), dtype=jnp.float32) * scale
        bias = jnp.zeros((L, D), dtype=jnp.float32)
        return {'x': x, 'edge_index': edge_index, 'edge_weight': edge_weight, 'W_self': W_self, 'W_neigh': W_neigh, 'bias': bias}
    _L1_gnn_all = _L1_gnn_setup()
    _L1_gnn_in = {k: v for k, v in _L1_gnn_all.items() if k in ('W_self', 'W_neigh', 'bias')}
    del _L1_gnn_all

    def _L2_gnn_setup():
        import jax, jax.numpy as jnp
        import numpy as np
        BN_EPS = 1e-05
        key = jax.random.key(seed)
        k_x, k_r, k_e, k_rel = jax.random.split(key, 4)
        e, E, dim, n_rels = (50000, 625000, 128, 1000)
        x = jax.random.normal(k_x, (e, dim), dtype=jnp.float32)
        r = jax.random.normal(k_r, (n_rels, dim), dtype=jnp.float32)
        gamma = jnp.ones((dim,), dtype=jnp.float32)
        beta = jnp.zeros((dim,), dtype=jnp.float32)
        kernels = jnp.ones((1, dim), dtype=jnp.float32)
        edges = jax.random.randint(k_e, (2, E), 0, e, dtype=jnp.int64)
        rels = jax.random.randint(k_rel, (E,), 0, n_rels, dtype=jnp.int64)
        return {'x': x, 'r': r, 'gamma': gamma, 'beta': beta, 'kernels': kernels, 'edges': edges, 'rels': rels}
    _L2_gnn_all = _L2_gnn_setup()
    _L2_gnn_in = {k: v for k, v in _L2_gnn_all.items() if k in ('r', 'gamma', 'beta', 'kernels')}
    del _L2_gnn_all

    def _L3_gnn_setup():
        import jax, jax.numpy as jnp
        import numpy as np
        import math
        N = 3125
        E = 31250
        D = 128
        ED = 16
        L = 5
        MID = 3
        ALPHA = 0.2
        THETA = 0.2
        NEG_SLOPE_ATT = 0.2

        def _gat_layer(x, src, dst, ea, W, We, a_src, a_dst, a_edge, b, n):
            h = x @ W
            e = ea @ We
            s = (h @ a_src)[src] + (h @ a_dst)[dst] + e @ a_edge
            s = jax.nn.leaky_relu(s, NEG_SLOPE_ATT)
            smax = jax.ops.segment_max(s, dst, num_segments=n)
            ex = jnp.exp(s - jax.lax.stop_gradient(smax)[dst])
            denom = jax.ops.segment_sum(ex, dst, num_segments=n)
            alpha = ex / denom[dst]
            out = jax.ops.segment_sum(h[src] * alpha[:, None], dst, num_segments=n)
            return out + b

        def _forward(x, edge_index, edge_attr, Ws, Wes, a_srcs, a_dsts, a_edges, biases, mid_ws):
            n = x.shape[0]
            src0, dst0 = (edge_index[0], edge_index[1])
            deg = jax.ops.segment_sum(jnp.ones_like(dst0, dtype=x.dtype), dst0, num_segments=n)
            loop_attr = jax.ops.segment_sum(edge_attr, dst0, num_segments=n) / jnp.clip(deg, 1.0)[:, None]
            loops = jnp.arange(n, dtype=src0.dtype)
            src = jnp.concatenate([src0, loops])
            dst = jnp.concatenate([dst0, loops])
            ea = jnp.concatenate([edge_attr, loop_attr], axis=0)
            x0 = _gat_layer(x, src, dst, ea, Ws[0], Wes[0], a_srcs[0], a_dsts[0], a_edges[0], biases[0], n)
            h = x0
            for i in range(MID):
                c = _gat_layer(h, src, dst, ea, Ws[i + 1], Wes[i + 1], a_srcs[i + 1], a_dsts[i + 1], a_edges[i + 1], biases[i + 1], n)
                beta = math.log(THETA / (i + 1) + 1.0)
                h = (1.0 - ALPHA) * c + ALPHA * x0
                h = (1.0 - beta) * h + beta * (h @ mid_ws[i])
                h = jax.nn.leaky_relu(h, 0.01)
            return _gat_layer(h, src, dst, ea, Ws[L - 1], Wes[L - 1], a_srcs[L - 1], a_dsts[L - 1], a_edges[L - 1], biases[L - 1], n)
        key = jax.random.key(seed)
        ks = jax.random.split(key, 10)
        s = 1.0 / np.sqrt(D)
        se = 1.0 / np.sqrt(ED)
        return {'x': jax.random.normal(ks[0], (N, D), jnp.float32), 'edge_index': jax.random.randint(ks[1], (2, E), 0, N, dtype=jnp.int64), 'edge_attr': jax.random.normal(ks[2], (E, ED), jnp.float32), 'Ws': jax.random.normal(ks[3], (L, D, D), jnp.float32) * s, 'Wes': jax.random.normal(ks[4], (L, ED, D), jnp.float32) * se, 'a_srcs': jax.random.normal(ks[5], (L, D), jnp.float32) * s, 'a_dsts': jax.random.normal(ks[6], (L, D), jnp.float32) * s, 'a_edges': jax.random.normal(ks[7], (L, D), jnp.float32) * s, 'biases': jnp.zeros((L, D), jnp.float32), 'mid_ws': jax.random.normal(ks[8], (MID, D, D), jnp.float32) * s}
    _L3_gnn_all = _L3_gnn_setup()
    _L3_gnn_in = {k: v for k, v in _L3_gnn_all.items() if k in ('Ws', 'Wes', 'a_srcs', 'a_dsts', 'a_edges', 'biases', 'mid_ws')}
    del _L3_gnn_all
    return {'x': x, 'src': src, 'dst': dst, 'edge_attr_16': edge_attr_16, 'edge_type_1000': edge_type_1000, 'edge_weight': edge_weight, 'L0_gnn_W': _L0_gnn_in['W'], 'L0_gnn_b': _L0_gnn_in['b'], 'L1_gnn_W_self': _L1_gnn_in['W_self'], 'L1_gnn_W_neigh': _L1_gnn_in['W_neigh'], 'L1_gnn_bias': _L1_gnn_in['bias'], 'L2_gnn_r': _L2_gnn_in['r'], 'L2_gnn_gamma': _L2_gnn_in['gamma'], 'L2_gnn_beta': _L2_gnn_in['beta'], 'L2_gnn_kernels': _L2_gnn_in['kernels'], 'L3_gnn_Ws': _L3_gnn_in['Ws'], 'L3_gnn_Wes': _L3_gnn_in['Wes'], 'L3_gnn_a_srcs': _L3_gnn_in['a_srcs'], 'L3_gnn_a_dsts': _L3_gnn_in['a_dsts'], 'L3_gnn_a_edges': _L3_gnn_in['a_edges'], 'L3_gnn_biases': _L3_gnn_in['biases'], 'L3_gnn_mid_ws': _L3_gnn_in['mid_ws']}

def reference(x, src, dst, edge_attr_16, edge_type_1000, edge_weight, L0_gnn_W, L0_gnn_b, L1_gnn_W_self, L1_gnn_W_neigh, L1_gnn_bias, L2_gnn_r, L2_gnn_gamma, L2_gnn_beta, L2_gnn_kernels, L3_gnn_Ws, L3_gnn_Wes, L3_gnn_a_srcs, L3_gnn_a_dsts, L3_gnn_a_edges, L3_gnn_biases, L3_gnn_mid_ws):
    import jax
    import jax.numpy as jnp

    def _L0_gnn_ref(x, source, target, W, b):
        import jax, jax.numpy as jnp
        import numpy as np
        N_NODES = 50000
        N_EDGES = 25000
        D_FEAT = 128
        UNITS = 128

        def _degree(idx, n_nodes):
            deg = jnp.zeros((n_nodes,), dtype=jnp.float32).at[idx].add(1.0)
            return jnp.maximum(deg, 1.0)
        n = x.shape[0]
        sender_scale = jax.lax.rsqrt(_degree(source, n))[:, None]
        receiver_scale = jax.lax.rsqrt(_degree(target, n))[:, None]
        normalized = sender_scale * x
        source_bcast = normalized[source]
        pooled = jax.ops.segment_sum(source_bcast, target, num_segments=n)
        pooled = receiver_scale * pooled
        return jax.nn.relu(pooled @ W + b)

    def _L1_gnn_ref(x, edge_index, edge_weight, W_self, W_neigh, bias):
        import jax, jax.numpy as jnp
        import numpy as np
        N = 3125
        E = 50000
        D = 128
        L = 2
        src, dst = (edge_index[0], edge_index[1])
        n = x.shape[0]
        deg = jax.ops.segment_sum(jnp.ones_like(edge_weight), dst, num_segments=n)
        deg = jnp.maximum(deg, 1.0)[:, None]
        nl = W_self.shape[0]
        for l in range(nl):
            msg = edge_weight[:, None] * x[src]
            agg = jax.ops.segment_sum(msg, dst, num_segments=n) / deg
            x = agg @ W_neigh[l] + x @ W_self[l] + bias[l]
            x = jax.nn.relu(x) if l < nl - 1 else jax.nn.sigmoid(x)
        return x

    def _L2_gnn_ref(x, r, gamma, beta, kernels, edges, rels):
        import jax, jax.numpy as jnp
        import numpy as np
        BN_EPS = 1e-05
        e, dim = x.shape
        mean = jnp.mean(x, axis=0)
        var = jnp.var(x, axis=0)
        x = (x - mean) * jax.lax.rsqrt(var + BN_EPS) * gamma + beta
        x = x * kernels
        r = r * kernels
        heads, tails = (edges[0], edges[1])
        head_emb = x[heads]
        rel_emb = r[rels]
        tail_emb = x[tails]
        receiver_emb = head_emb + rel_emb
        sender_emb = tail_emb - rel_emb
        sum_in = jax.ops.segment_sum(receiver_emb, tails, num_segments=e)
        sum_out = jax.ops.segment_sum(sender_emb, heads, num_segments=e)
        du = jnp.ones((e,), dtype=jnp.float32)
        for row in (heads, rels, tails):
            inc = (row[0] != row[2]).astype(jnp.float32)
            du = du.at[row[0]].add(inc)
            du = du.at[row[2]].add(inc)
        return (sum_out + sum_in + x) / du[:, None]

    def _L3_gnn_ref(x, edge_index, edge_attr, Ws, Wes, a_srcs, a_dsts, a_edges, biases, mid_ws):
        import jax, jax.numpy as jnp
        import numpy as np
        import math
        N = 3125
        E = 31250
        D = 128
        ED = 16
        L = 5
        MID = 3
        ALPHA = 0.2
        THETA = 0.2
        NEG_SLOPE_ATT = 0.2

        def _gat_layer(x, src, dst, ea, W, We, a_src, a_dst, a_edge, b, n):
            h = x @ W
            e = ea @ We
            s = (h @ a_src)[src] + (h @ a_dst)[dst] + e @ a_edge
            s = jax.nn.leaky_relu(s, NEG_SLOPE_ATT)
            smax = jax.ops.segment_max(s, dst, num_segments=n)
            ex = jnp.exp(s - jax.lax.stop_gradient(smax)[dst])
            denom = jax.ops.segment_sum(ex, dst, num_segments=n)
            alpha = ex / denom[dst]
            out = jax.ops.segment_sum(h[src] * alpha[:, None], dst, num_segments=n)
            return out + b

        def _forward(x, edge_index, edge_attr, Ws, Wes, a_srcs, a_dsts, a_edges, biases, mid_ws):
            n = x.shape[0]
            src0, dst0 = (edge_index[0], edge_index[1])
            deg = jax.ops.segment_sum(jnp.ones_like(dst0, dtype=x.dtype), dst0, num_segments=n)
            loop_attr = jax.ops.segment_sum(edge_attr, dst0, num_segments=n) / jnp.clip(deg, 1.0)[:, None]
            loops = jnp.arange(n, dtype=src0.dtype)
            src = jnp.concatenate([src0, loops])
            dst = jnp.concatenate([dst0, loops])
            ea = jnp.concatenate([edge_attr, loop_attr], axis=0)
            x0 = _gat_layer(x, src, dst, ea, Ws[0], Wes[0], a_srcs[0], a_dsts[0], a_edges[0], biases[0], n)
            h = x0
            for i in range(MID):
                c = _gat_layer(h, src, dst, ea, Ws[i + 1], Wes[i + 1], a_srcs[i + 1], a_dsts[i + 1], a_edges[i + 1], biases[i + 1], n)
                beta = math.log(THETA / (i + 1) + 1.0)
                h = (1.0 - ALPHA) * c + ALPHA * x0
                h = (1.0 - beta) * h + beta * (h @ mid_ws[i])
                h = jax.nn.leaky_relu(h, 0.01)
            return _gat_layer(h, src, dst, ea, Ws[L - 1], Wes[L - 1], a_srcs[L - 1], a_dsts[L - 1], a_edges[L - 1], biases[L - 1], n)
        return _forward(x, edge_index, edge_attr, Ws, Wes, a_srcs, a_dsts, a_edges, biases, mid_ws)
    edge_index = jnp.stack([src, dst])
    h = jnp.maximum(_layernorm(x, axis=-1), 0.0)
    x = x + _L0_gnn_ref(h, src, dst, L0_gnn_W, L0_gnn_b)
    h = jnp.maximum(_layernorm(x, axis=-1), 0.0)
    x = x + _L1_gnn_ref(h, edge_index, edge_weight, L1_gnn_W_self, L1_gnn_W_neigh, L1_gnn_bias)
    h = jnp.maximum(_layernorm(x, axis=-1), 0.0)
    x = x + _L2_gnn_ref(h, L2_gnn_r, L2_gnn_gamma, L2_gnn_beta, L2_gnn_kernels, edge_index, edge_type_1000)
    h = jnp.maximum(_layernorm(x, axis=-1), 0.0)
    x = x + _L3_gnn_ref(h, edge_index, edge_attr_16, L3_gnn_Ws, L3_gnn_Wes, L3_gnn_a_srcs, L3_gnn_a_dsts, L3_gnn_a_edges, L3_gnn_biases, L3_gnn_mid_ws)
    return x

_drawn_inputs = setup_inputs


def setup_inputs(seed=0):
    import zlib

    import numpy as np

    out = dict(_drawn_inputs(seed))
    spreads = {'L0_gnn_b': (0.0, 0.1),
     'L1_gnn_bias': (0.0, 0.608),
     'L2_gnn_gamma': (1.0, 0.2),
     'L2_gnn_beta': (0.0, 0.1),
     'L2_gnn_kernels': (1.0, 0.2),
     'L3_gnn_biases': (0.0, 0.8)}
    factors = {'edge_attr_16': 8.0,
     'edge_weight': 8.0,
     'L3_gnn_Ws': 8.0,
     'L3_gnn_Wes': 8.0,
     'L3_gnn_a_srcs': 8.0,
     'L3_gnn_a_dsts': 8.0,
     'L3_gnn_a_edges': 8.0,
     'L3_gnn_mid_ws': 8.0}
    for name, (base, spread) in spreads.items():
        noise = np.random.default_rng([zlib.crc32(name.encode()), seed]).standard_normal(out[name].shape)
        drawn = base * np.exp(spread * noise) if base else spread * noise
        out[name] = jnp.asarray(drawn.astype(out[name].dtype))
    for name, factor in factors.items():
        out[name] = (out[name] * factor).astype(out[name].dtype)
    return out
```

```python
from contextlib import ExitStack
import math

import numpy as np
import concourse.bass as bass
from concourse import mybir

F32, I32, U32, BF16 = mybir.dt.float32, mybir.dt.int32, mybir.dt.uint32, mybir.dt.bfloat16
ALU = mybir.AluOpType
ACT = mybir.ActivationFunctionType
AX_X = mybir.AxisListType.X

P = 128
D = 128
BIG = 1e38
RW = 12
F_SRC, F_DST, F_TYPE, F_W, F_VALID, F_C = 0, 1, 2, 3, 4, 5
GT = 8
ST = 4
SCAN_C = 7
ALPHA, THETA, ATT_SLOPE, OUT_SLOPE, EPS = 0.2, 0.2, 0.2, 0.01, 1e-5


def ceil_to(x, m):
    return -(-x // m) * m


def build(nc, a, out):
    x_in, W0 = a["x"], a["L0_gnn_W"]
    N = x_in.shape[0]
    E = a["src"].shape[0]
    ED = a["edge_attr_16"].shape[1]
    R = a["L2_gnn_r"].shape[0]
    NL = a["L3_gnn_Ws"].shape[0]
    MID = a["L3_gnn_mid_ws"].shape[0]
    NB = -(-N // P)
    TAIL = N - (NB - 1) * P
    EP = 125
    EC = E // EP
    assert EP * EC == E and EC % (2 * ST) == 0 and EC % GT == 0 and R % EP == 0
    EA_CHUNKS = 4
    EA_COLS = EC // EA_CHUNKS
    assert EA_COLS * EA_CHUNKS == EC and EA_COLS % (2 * ST) == 0 and GT == 2 * ST
    ITEMS = E + N
    NT_LOW = ceil_to(EC + NB, 2 * ST)
    NT_HIGH = ceil_to(-(-ITEMS // P), 2 * ST)
    NT_D = ceil_to((ITEMS + NB * (P - 1)) // P, 2 * GT)
    NT_S = ceil_to((E + NB * (P - 1)) // P, 2 * GT)
    NT_A = P * SCAN_C
    assert NT_D + GT <= NT_A and NT_S <= NT_D and NT_HIGH <= NT_D and NT_LOW <= NT_D
    DUMP = NT_D * P
    SPARE = 2 * DUMP
    ROWS = SPARE + 2 * ST
    BLANKS = 8
    BLANK_T = NT_D // BLANKS
    assert BLANK_T * BLANKS == NT_D
    SQ = SCAN_C * P
    BATCHES = [(b, min(4, NB - b)) for b in range(0, NB, 4)]
    NBT = len(BATCHES)

    def scratch(name, shape, dt):
        return nc.dram_tensor(name, shape, dt, kind="Internal").ap()

    rec_low = scratch("rec_low", (ROWS, RW), F32)
    rec_dst = scratch("rec_dst", (ROWS, RW), F32)
    rec_src = scratch("rec_src", (ROWS, RW), F32)
    table = scratch("table", (NB * P, D), F32)
    table_r = scratch("table_r", (R, D), F32)
    srclo_d = scratch("srclo_d", (P * SQ,), BF16)
    dstlo_d = scratch("dstlo_d", (P * SQ,), BF16)
    dst_d = scratch("dst_d", (P * SQ + 2,), F32)

    SORTS = [(EC, NB, rec_src), (NT_LOW, P, rec_low), (NT_HIGH, NB, rec_dst)]
    sort_base = [0]
    for nt, _, _ in SORTS:
        sort_base.append(sort_base[-1] + nt // ST)
    PASSES = [("dst", "valid", True, True), ("dst", "w", True, True), ("dst", "w", True, True),
              ("dst", "valid", True, False), ("dst_rel", "valid", False, False),
              ("src", "valid", False, False), ("src_rel", "neg", False, True)]
    PASSES += [("dst", "alpha", True, True)] * NL
    pass_base = [0]
    for kind, _, _, _ in PASSES:
        pass_base.append(pass_base[-1] + (NT_D if kind[:3] == "dst" else NT_S) // GT)
    DENSE = [1, 2, 2] + [1] * (NL + MID)
    dense_t, dense_b = [0], [0]
    for n in DENSE:
        dense_t.append(dense_t[-1] + n * NBT)
        dense_b.append(dense_b[-1] + NBT)

    def m_rows(l):
        return 3 if l == 0 else 2 + 2 * l

    def m_mid(l):
        return 3 + 2 * l

    SG = NT_D // GT

    with ExitStack() as ctx:
        def sb(name, shape, dt=F32):
            return ctx.enter_context(nc.sbuf_tensor(name, shape, dt))

        def sem(name):
            return ctx.enter_context(nc.semaphore(name))

        ps = ctx.enter_context(nc.psum_tensor("ps", [P, 8, 512], F32))
        psf = ps[:].rearrange("p b c -> p (b c)")
        acc = psf[:, 0:NB * D]

        X = sb("X", [P, NB, D])
        H = sb("H", [P, NB, D])
        AGG = sb("AGG", [P, NB, D])
        TA = sb("TA", [P, NB, D])
        TB = sb("TB", [P, NB, D])
        REC = sb("REC", [P, NT_D, RW])
        X0 = H

        pid_i = sb("pid_i", [P, 1], I32)
        col_f = sb("col_f", [P, NT_A])
        pid_f = sb("pid_f", [P, 1])
        dump_f = sb("dump_f", [P, 1])
        ident = sb("ident", [P, P])
        before_f = sb("before_f", [P, P])
        ones_f = sb("ones_f", [P, P])
        before = sb("before", [P, P], BF16)
        not_before = sb("not_before", [P, P], BF16)
        ones = sb("ones", [P, P], BF16)
        zeros = sb("zeros", [P, 512], BF16)
        node_id = sb("node_id", [P, NB])
        is_node = sb("is_node", [P, NB])
        guard = sb("guard", [1, 1])

        w0 = sb("w0", [P, D])
        w_self = sb("w_self", [P, 2, D])
        w_neigh = sb("w_neigh", [P, 2, D])
        w_gat = sb("w_gat", [P, NL, D])
        w_mid = sb("w_mid", [P, MID, D])
        b0 = sb("b0", [P, D])
        b1 = sb("b1", [P, 2, D])
        gamma = sb("gamma", [P, D])
        beta = sb("beta", [P, D])
        kern = sb("kern", [P, D])
        a_src = sb("a_src", [P, NL, D])
        a_dst = sb("a_dst", [P, NL, D])
        b3 = sb("b3", [P, NL, D])
        firsts_i = sb("firsts_i", [P, 3, 3], I32)
        firsts = sb("firsts", [P, 3, 3])

        deg_dst = sb("deg_dst", [P, NB])
        deg_src = sb("deg_src", [P, NB])
        rdeg = sb("rdeg", [P, NB])
        rs_dst = sb("rs_dst", [P, NB])
        rs_src = sb("rs_src", [P, NB])
        cnt = sb("cnt", [P, NB])
        col1 = sb("col1", [P, 1])
        base_col = sb("base_col", [P, P])
        base = sb("base", [P, 3, P])
        tiles_of = sb("tiles_of", [P, NB])
        tiles_i = sb("tiles_i", [P, NB], I32)
        tiles_end = sb("tiles_end", [P, 2, NB])
        blk_d = sb("blk_d", [1, NT_A], I32)
        blk_s = sb("blk_s", [1, NT_A], I32)
        smallA = sb("smallA", [P, NB])
        smallB = sb("smallB", [P, NB])
        smallC = sb("smallC", [P, NB])
        bn_tmp = sb("bn_tmp", [P, D])
        vcol = sb("vcol", [P, 1])
        vproj = sb("vproj", [P, NL * ED])
        posf = sb("posf", [P, 2, ST])
        inv = sb("inv", [P, 2, ST])
        pos_ring = sb("pos_ring", [P, 2, ST], U32)
        rec_ring = sb("rec_ring", [P, 2, ST, RW])
        oh_ring = sb("oh_ring", [P, 2, ST, P], BF16)

        oh_shi_t = sb("oh_shi_t", [P, GT, NB], BF16)
        ends_col = sb("ends_col", [NB, 2])
        bn_row = sb("bn_row", [P, D])

        t_src = sb("t_src", [P, NT_D], U32)
        t_type = sb("t_type", [P, NT_D], U32)
        t_lo = sb("t_lo", [P, NT_A])
        t_w = sb("t_w", [P, NT_D])
        t_valid = sb("t_valid", [P, NT_D])
        t_c = sb("t_c", [P, NL, NT_D])
        t_hi = sb("t_hi", [P, NT_D, 2])
        t_alpha = sb("t_alpha", [P, NT_A])

        idx_ring = sb("idx_ring", [P, 2, GT], U32)
        row_ring = sb("row_ring", [P, 2, GT, D])
        dw_ring = sb("dw_ring", [P, 2, GT, P])
        xt_ring = sb("xt_ring", [P, 2, 512])
        carry_row = sb("carry_row", [1, P + 2])
        row_a = sb("row_a", [1, P])
        row_b = sb("row_b", [1, P])
        carry_col = sb("carry_col", [P, 1])
        keep_rows = sb("keep_rows", [1, 3, P])
        hs_parts = sb("hs_parts", [P, 3, NB], BF16)
        hd_parts = sb("hd_parts", [P, 3, NB], BF16)

        recf = REC[:].rearrange("p t w -> p (t w)")
        def scan_view(i):
            return recf[:, i * SQ:(i + 1) * SQ]
        sc_score, sc_fwd, sc_ends, sc_tot, sc_ex = (scan_view(i) for i in range(5))
        sc_neg, sc_keepf, sc_keepb, sc_end = (scan_view(i) for i in range(5, 9))
        flat = lambda t: t[:].rearrange("p b d -> p (b d)")
        s_found = [flat(TA)[:, i * NT_D:i * NT_D + NT_S] for i in range(3)] + [
            flat(TB)[:, i * NT_D:i * NT_D + NT_S] for i in (1, 2)]
        s_kept = [scan_view(i)[:, 0:NT_S] for i in range(5)]
        s_dst, s_type = (t.bitcast(U32) for t in s_kept[0:2])
        s_lo, s_valid, s_neg = s_kept[2:5]
        key = flat(TA)[:, 0:NT_D + 2 * ST]
        t_srclo = flat(AGG)[:, 2048:2048 + NT_A]
        past = flat(TB)[0:NB, 2304:2304 + NT_A].bitcast(BF16).rearrange("b (s t) -> b s t", t=NT_A)
        col_i = flat(TB)[:, 0:NT_A].bitcast(I32)
        src_i = flat(TA)[0:EP, 0:EC].bitcast(I32)
        dst_i = flat(TA)[0:EP, EC:2 * EC].bitcast(I32)
        type_i = flat(TA)[0:EP, 2 * EC:3 * EC].bitcast(I32)
        w_in = flat(TA)[0:EP, 3 * EC:4 * EC]
        assert 3 * NT_D <= NB * D and 2048 + NT_A <= NB * D and 2304 + NT_A <= NB * D
        assert 4 * EC <= NB * D and EA_COLS * ED <= min(NB * D, NL * NT_D)
        ea = [t[0:EP, 0:EA_COLS * ED].rearrange("p (t k) -> p t k", k=ED)
              for t in (flat(H), t_c[:].rearrange("p l t -> p (l t)"), flat(X), flat(AGG))]
        ea_prod = flat(TB)[0:EP, 1024:1024 + NL * GT * ED].rearrange("p (l t k) -> p l t k", l=NL, k=ED)
        src_eq = flat(TB)[0:EP, 0:4 * EC].rearrange("p (b t) -> p b t", t=EC)
        blank = flat(AGG)[:, 0:BLANK_T * RW].rearrange("p (t w) -> p t w", w=RW)
        wes = flat(AGG)[0:NL * ED, 1600:1600 + D]
        aedge = flat(AGG)[0:NL * ED, 1600 + D:1600 + 2 * D]
        aprod = flat(AGG)[0:NL * ED, 1600 + 2 * D:1600 + 3 * D]
        lo_dst, hi_dst, lo_src, hi_src = (t[0:EP, 0:EC] for t in (t_lo, t_type[:].bitcast(F32), t_w, t_valid))
        dig_i = t_alpha[0:EP, 0:EC].bitcast(I32)
        oh_dlo = dw_ring[0:EP, 0]
        oh_slo = dw_ring[0:EP, 1].rearrange("p a b -> p (a b)").bitcast(BF16)[:, 0:GT * P].rearrange("p (t c) -> p t c", c=P)
        oh_dhi = row_ring[0:EP].rearrange("p a b d -> p (a b d)")[:, 0:GT * 6 * NB].rearrange(
            "p (t l c) -> p t l c", l=6, c=NB)
        oh_shi = oh_shi_t[0:EP]
        relr = flat(AGG)[0:EP, 0:R // EP * D].rearrange("p (t d) -> p t d", d=D)
        rank_prod = TB[:, 0:ST, :]
        lo_ring = row_ring[:].rearrange("p a b d -> p (a b d)").bitcast(BF16).rearrange(
            "p (h s c) -> p h s c", h=2, s=2)
        oht_ring = dw_ring[:].rearrange("p a b d -> p (a b d)").bitcast(BF16).rearrange(
            "p (h s c) -> p h s c", h=2, s=2)
        oh_hi = flat(TB)[:, 0:GT * 2 * NB].rearrange("p (t s c) -> p t s c", s=2, c=NB)
        pr_hi = flat(TB)[:, 512:512 + GT * 2 * NB].rearrange("p (t c) -> p t c", c=2 * NB)

        idx_of = {"dst": t_src, "dst_rel": t_type, "src": s_dst, "src_rel": s_type}
        wt_of = {("dst", "valid"): t_valid, ("dst", "w"): t_w, ("dst", "alpha"): t_alpha,
                 ("src", "valid"): s_valid, ("src", "neg"): s_neg}

        def tiles_bank(t):
            return psf[:, t * 1024:(t + 1) * 1024].rearrange("p (j c) -> p j c", c=P)

        iotas = sem("iotas")
        consts_ready = sem("consts_ready")
        x_cleared = sem("x_cleared")
        x_loaded = sem("x_loaded")
        edges_loaded = sem("edges_loaded")
        weights_loaded = sem("weights_loaded")
        blank_ready = sem("blank_ready")
        blanked = sem("blanked")
        attr_loaded = [sem(f"attr_loaded{i}") for i in range(EA_CHUNKS)]
        vcol_ready = sem("vcol_ready")
        vproj_ready = sem("vproj_ready")
        dst_onehots = sem("dst_onehots")
        src_onehots = sem("src_onehots")
        dst_multiplied = sem("dst_multiplied")
        src_multiplied = sem("src_multiplied")
        ends_ready = sem("ends_ready")
        blocks_found = sem("blocks_found")
        counts_ready = sem("counts_ready")
        counts_summed = sem("counts_summed")
        sort_ready = sem("sort_ready")
        onehot_ready = sem("onehot_ready")
        prefix_ready = sem("prefix_ready")
        prefix_read = sem("prefix_read")
        pos_ready = sem("pos_ready")
        rec_staged = sem("rec_staged")
        scattered = [sem(f"scattered{i}") for i in range(2)]
        rec_loaded = sem("rec_loaded")
        rec_free = sem("rec_free")
        layout_src = sem("layout_src")
        layout_done = sem("layout_done")
        layout_read = sem("layout_read")
        slot_rows = sem("slot_rows")
        slot_stored = sem("slot_stored")
        dst_stored = sem("dst_stored")
        neigh_loaded = sem("neigh_loaded")
        var_ready = sem("var_ready")
        std_ready = sem("std_ready")
        table_rows = sem("table_rows")
        table_written = sem("table_written")
        rel_loaded = sem("rel_loaded")
        rel_rows = sem("rel_rows")
        idx_staged = sem("idx_staged")
        landed = [[sem(f"landed{s}_{i}") for i in range(2)] for s in range(2)]
        LANDED_SPLIT = 6
        weights_ready = sem("weights_ready")
        tiles_done = sem("tiles_done")
        pass_ready = sem("pass_ready")
        dense_src = sem("dense_src")
        turned = sem("turned")
        turned_copied = sem("turned_copied")
        turned_used = sem("turned_used")
        dense_read = sem("dense_read")
        gate_in = sem("gate_in")
        gate_out = sem("gate_out")
        bn_src = sem("bn_src")
        bn_sum = sem("bn_sum")
        parts_ready = sem("parts_ready")
        lo_landed = [sem(f"lo_landed{i}") for i in range(2)]
        oht_ready = sem("oht_ready")
        score_mm = sem("score_mm")
        score_read = sem("score_read")
        carry_in = sem("carry_in")
        carry_t = sem("carry_t")
        exp_in = sem("exp_in")
        exp_out = sem("exp_out")
        final_rows = sem("final_rows")
        out_written = sem("out_written")

        NCONST = 2
        block = ctx.enter_context(nc.Block())

        @block.sync
        def _(sp):
            for view, name in ((src_i, "src"), (dst_i, "dst"), (type_i, "edge_type_1000"), (w_in, "edge_weight")):
                sp.dma_start(view, a[name].rearrange("(p t) -> p t", p=EP)).then_inc(edges_loaded, 16)
            sp.dma_start(wes, a["L3_gnn_Wes"].rearrange("l k d -> (l k) d")).then_inc(weights_loaded, 16)
            for l in range(NL):
                sp.dma_start(aedge[l * ED:(l + 1) * ED, :],
                             a["L3_gnn_a_edges"][l, :].partition_broadcast(ED)).then_inc(weights_loaded, 16)
            attr = a["edge_attr_16"].rearrange("(p t) k -> p t k", p=EP)
            for i in range(EA_CHUNKS):
                if i == EA_CHUNKS - 1:
                    sp.wait_ge(vcol_ready, 1)
                    sp.wait_ge(blanked, 16 * 3 * BLANKS)
                    for h in range(2):
                        sp.wait_ge(scattered[h], 16 * ST)
                sp.dma_start(ea[i], attr[:, i * EA_COLS:(i + 1) * EA_COLS, :]).then_inc(attr_loaded[i], 16)
            sp.wait_ge(x_cleared, 1)
            sp.dma_start(X[:, 0:NB - 1, :], x_in[0:(NB - 1) * P, :].rearrange("(b p) f -> p b f", p=P)).then_inc(x_loaded, 16)
            sp.dma_start(X[0:TAIL, NB - 1, :], x_in[(NB - 1) * P:N, :]).then_inc(x_loaded, 16)

            n = sort_base[2] // 2
            for h in range(2):
                sp.wait_ge(scattered[h], 16 * ST * (n + 1))
            sp.dma_start(REC[:, 0:NT_HIGH, :],
                         rec_low[0:NT_HIGH * P, :].rearrange("(t q) w -> q t w", q=P)).then_inc(rec_loaded, 16)
            n = sort_base[3] // 2
            for h in range(2):
                sp.wait_ge(scattered[h], 16 * ST * (n + 1))
            sp.dma_start(REC[:, 0:NT_D, :],
                         rec_dst[0:NT_D * P, :].rearrange("(t q) w -> q t w", q=P)).then_inc(rec_loaded, 16)
            sp.wait_ge(rec_free, 1)
            sp.dma_start(REC[:, 0:NT_S, :],
                         rec_src[0:NT_S * P, :].rearrange("(t q) w -> q t w", q=P)).then_inc(rec_loaded, 16)

            sp.wait_ge(slot_rows, 1)
            sp.dma_start(dst_d[1:1 + P * SQ].rearrange("(p j) -> p j", p=P), sc_score).then_inc(dst_stored, 16)
            sp.dma_start(dst_d[0:1].rearrange("(p j) -> p j", p=1), guard[:, :]).then_inc(dst_stored, 16)
            sp.dma_start(dst_d[1 + P * SQ:2 + P * SQ].rearrange("(p j) -> p j", p=1), guard[:, :]).then_inc(dst_stored, 16)
            for i, dram in enumerate((srclo_d, dstlo_d)):
                sp.wait_ge(slot_rows, 2 + i)
                sp.dma_start(dram.rearrange("(p j) -> p j", p=P), scan_view(1 + i).bitcast(BF16)[:, 0:SQ]).then_inc(slot_stored, 16)
            sp.wait_ge(dst_stored, 16 * 3)
            sp.dma_start(sc_tot, dst_d[0:P * SQ].rearrange("(p j) -> p j", p=P)).then_inc(neigh_loaded, 16)
            sp.dma_start(sc_ex, dst_d[2:2 + P * SQ].rearrange("(p j) -> p j", p=P)).then_inc(neigh_loaded, 16)
            sp.wait_ge(slot_stored, 16 * 2)

            def store_table(k, rows):
                sp.wait_ge(table_rows, k + 1)
                sp.dma_start(table.rearrange("(b p) f -> p b f", p=P), rows[:, :, :]).then_inc(table_written, 16)

            store_table(0, AGG)
            store_table(1, H)
            store_table(2, TA)
            sp.wait_ge(gate_in, 1)
            sp.dma_start(relr, a["L2_gnn_r"].rearrange("(p t) d -> p t d", p=EP)).then_inc(rel_loaded, 16)
            sp.wait_ge(rel_rows, 1)
            sp.dma_start(table_r.rearrange("(p t) d -> p t d", p=EP), relr).then_inc(table_written, 16)
            store_table(3, H)
            for l in range(NL):
                store_table(4 + l, TA)
                first = l * (SG + 1)
                def lo_group(g, h, ready):
                    sp.wait_ge(oht_ready, ready)
                    for s, dram in enumerate((srclo_d, dstlo_d)):
                        sp.dma_start(lo_ring[:, h, s, :],
                                     dram[bass.ds(g * GT * P, GT * P)].partition_broadcast(P)).then_inc(lo_landed[h], 16)
                sp.wait_ge(parts_ready, l + 1)
                with sp.Fori(0, SG // 2) as i:
                    for h in range(2):
                        lo_group(i * 2 + h, h, i * 2 + (first + h + 1))
                lo_group(SG, 0, first + SG + 1)
            sp.wait_ge(final_rows, 1)
            sp.dma_start(out[0:(NB - 1) * P, :].rearrange("(b p) f -> p b f", p=P), X[:, 0:NB - 1, :]).then_inc(out_written, 16)
            sp.dma_start(out[(NB - 1) * P:N, :], X[0:TAIL, NB - 1, :]).then_inc(out_written, 16)
            sp.wait_ge(out_written, 32)

        @block.scalar
        def _(act):
            loads = [(w0[:], W0), (w_self[:], a["L1_gnn_W_self"].rearrange("l k d -> k l d")),
                     (w_neigh[:], a["L1_gnn_W_neigh"].rearrange("l k d -> k l d")),
                     (w_gat[:], a["L3_gnn_Ws"].rearrange("l k d -> k l d")),
                     (w_mid[:], a["L3_gnn_mid_ws"].rearrange("l k d -> k l d")),
                     (b0[:], a["L0_gnn_b"].partition_broadcast(P)),
                     (gamma[:], a["L2_gnn_gamma"].partition_broadcast(P)),
                     (beta[:], a["L2_gnn_beta"].partition_broadcast(P)),
                     (kern[:], a["L2_gnn_kernels"].rearrange("o d -> (o d)").partition_broadcast(P)),
                     (b1[:].rearrange("p l d -> p (l d)"), a["L1_gnn_bias"].rearrange("l d -> (l d)").partition_broadcast(P)),
                     (a_src[:].rearrange("p l d -> p (l d)"), a["L3_gnn_a_srcs"].rearrange("l d -> (l d)").partition_broadcast(P)),
                     (a_dst[:].rearrange("p l d -> p (l d)"), a["L3_gnn_a_dsts"].rearrange("l d -> (l d)").partition_broadcast(P)),
                     (b3[:].rearrange("p l d -> p (l d)"), a["L3_gnn_biases"].rearrange("l d -> (l d)").partition_broadcast(P))]
            for k, name in enumerate(("src", "dst", "edge_type_1000")):
                loads.append((firsts_i[:, k, :], a[name][0:3].partition_broadcast(P)))
            for dst, src in loads:
                act.dma_start(dst, src).then_inc(weights_loaded, 16)
            act.wait_ge(blank_ready, 1)
            for rec in (rec_low, rec_dst, rec_src):
                rows = rec[0:DUMP, :].rearrange("(p c t) w -> p c t w", p=P, t=BLANK_T)
                for c in range(BLANKS):
                    act.dma_start(rows[:, c], blank).then_inc(blanked, 16)

            act.preload_act_table(ACT.Copy)
            for k, (nt, _, _) in enumerate(SORTS):
                act.wait_ge(sort_ready, k + 1)
                b = sort_base[k] // 2
                words = F_C if k == 0 else RW
                with act.Fori(0, nt // (2 * ST)) as i:
                    for h in range(2):
                        act.wait_ge(scattered[h], i * (16 * ST) + 16 * ST * (b + 1))
                        nc.scalar.copy(rec_ring[:, h, :, 0:words], REC[:, bass.ds((i * 2 + h) * ST, ST), 0:words]).then_inc(rec_staged, 1)

            def sqrt_step(k, t):
                act.wait_ge(var_ready, k + 1)
                nc.scalar.activation(t, t, ACT.Sqrt).then_inc(std_ready, 1)

            def copy_turned(m):
                for j in range(DENSE[m] * NBT):
                    t = dense_t[m] + j
                    n = BATCHES[j // DENSE[m]][1] * P
                    act.wait_ge(turned, t + 1)
                    if t >= 2:
                        act.wait_ge(turned_used, t - 1)
                    nc.scalar.copy(xt_ring[:, t % 2, 0:n], ps[:, t % 2, 0:n]).then_inc(turned_copied, 1)

            def stage_indices(k0, k1):
                for k in range(k0, k1):
                    kind = PASSES[k][0]
                    g0 = pass_base[k]
                    act.wait_ge(pass_ready, k + 1)
                    with act.Fori(0, (pass_base[k + 1] - g0) // 2) as i:
                        for h in range(2):
                            act.wait_ge(tiles_done, i * 2 + (g0 + h + 1))
                            nc.scalar.copy(idx_ring[:, h, :], idx_of[kind][:, bass.ds((i * 2 + h) * GT, GT)]).then_inc(idx_staged, 1)

            sqrt_step(0, smallB[:])
            sqrt_step(1, rs_dst[:])
            sqrt_step(2, rs_src[:])
            stage_indices(0, 1)
            copy_turned(0)
            sqrt_step(3, smallB[:])
            stage_indices(1, 2)
            copy_turned(1)
            stage_indices(2, 3)
            copy_turned(2)
            act.wait_ge(gate_in, 1)
            nc.scalar.activation(flat(TA), flat(TA), ACT.Exp, scale=-1.0).then_inc(gate_out, 1)
            sqrt_step(4, smallB[:])
            sqrt_step(5, bn_row[:])
            stage_indices(3, 7)
            sqrt_step(6, smallB[:])
            for l in range(NL):
                copy_turned(m_rows(l))
                act.wait_ge(exp_in, l + 1)
                nc.scalar.activation(sc_ex, sc_ex, ACT.Exp).then_inc(exp_out, 1)
                stage_indices(7 + l, 8 + l)
                if 1 <= l <= MID:
                    copy_turned(m_mid(l))

        @block.gpsimd
        def _(pool):
            nc.gpsimd.iota(col_i[:], [[1, NT_A]], base=0, channel_multiplier=0).then_inc(iotas, 1)
            nc.gpsimd.iota(pid_i[:], [[0, 1]], base=0, channel_multiplier=1).then_inc(iotas, 1)

            group = pool.alloc_register("group")
            pool.reg_mov(group, 0)
            pool.wait_ge(blanked, 16 * 3 * BLANKS)
            for h in range(2):
                pool.dma_start(rec_low[SPARE + h * ST:SPARE + (h + 1) * ST, :], blank[0:ST, 0, :]).then_inc(scattered[h], 16 * ST)
            for k, (nt, _, rec) in enumerate(SORTS):
                g0 = sort_base[k]
                with pool.Fori(0, nt // (2 * ST)) as i:
                    for h in range(2):
                        pool.reg_add(group, group, 1)
                        pool.wait_ge(sort_ready, k + 1)
                        pool.wait_ge(pos_ready, group)
                        pool.wait_ge(rec_staged, group)
                        for j in range(ST):
                            pool.indirect_dma_start(
                                rec, bass.IndirectOffsetOnAxis(ap=pos_ring[:, h, j:j + 1], axis=0),
                                rec_ring[:, h, j, :], None).then_inc(scattered[h], 16)

            pool.reg_mov(group, 0)
            tables = 0
            for k, (kind, _, clears, _) in enumerate(PASSES):
                if kind == "dst":
                    tables += 1
                    pool.wait_ge(pass_ready, k + 1)
                arrived = landed[k >= LANDED_SPLIT]
                tab = table_r if kind.endswith("rel") else table
                g0 = pass_base[k]
                with pool.Fori(0, (pass_base[k + 1] - g0) // 2) as i:
                    for h in range(2):
                        pool.reg_add(group, group, 1)
                        pool.wait_ge(table_written, 16 * (tables + (1 if tables > 3 else 0)))
                        pool.wait_ge(idx_staged, group)
                        for j in range(GT):
                            pool.indirect_dma_start(
                                row_ring[:, h, j, :], None, tab,
                                bass.IndirectOffsetOnAxis(ap=idx_ring[:, h, j:j + 1], axis=0)).then_inc(arrived[h], 16)

        @block.tensor
        def _(pe):
            pe.wait_ge(vcol_ready, 1)
            KE = NL * ED
            nc.tensor.transpose(ps[0:P, 7, 0:KE], base_col[0:KE, :], ident[0:KE, 0:KE]).then_inc(vproj_ready, 1)

            def dst_degrees(i):
                pe.wait_ge(dst_onehots, i + 1)
                for j in range(GT):
                    mm = nc.tensor.matmul(ps[:, 0, 0:6 * NB], oh_dlo[:, j, :], oh_dhi[:, j, :, :].rearrange("p l c -> p (l c)"),
                                          start=False, stop=False, skip_group_check=True)
                mm.then_inc(dst_multiplied, 1)

            def src_degrees(i):
                pe.wait_ge(src_onehots, i + 1)
                for j in range(GT):
                    mm = nc.tensor.matmul(ps[:, 1, 0:NB], oh_slo[:, j, :], oh_shi[:, j, :],
                                          start=False, stop=False, skip_group_check=True)
                mm.then_inc(src_multiplied, 1)

            nc.tensor.matmul(ps[:, 0, :], ones[:], zeros[:], start=True, stop=False, skip_group_check=True).then_inc(dst_multiplied, 1)
            nc.tensor.matmul(ps[:, 1, :], ones[:], zeros[:], start=True, stop=False, skip_group_check=True)

            pe.wait_ge(counts_ready, 1)
            nc.tensor.matmul(ps[:, 4, 0:NB], ones_f[:], cnt[:], start=True, stop=True).then_inc(counts_summed, 1)

            for k, (nt, bins, _) in enumerate(SORTS):
                g0 = sort_base[k]
                if k == 1:
                    src_degrees(EC // GT)
                    pe.wait_ge(counts_ready, 2)
                    nc.tensor.matmul(ps[:, 2, 0:1], before_f[:], col1[:], start=True, stop=True)
                    nc.tensor.matmul(ps[:, 3, 0:NB], ones_f[:], cnt[:], start=True, stop=True).then_inc(counts_summed, 1)
                    pe.wait_ge(counts_ready, 3)
                    nc.tensor.transpose(ps[:, 5, 0:P], base_col[:], ident[:]).then_inc(counts_summed, 1)
                    pe.wait_ge(ends_ready, 1)
                    for q in range(2):
                        mm = nc.tensor.transpose(ps[0:NB, 3, q * P:(q + 1) * P], tiles_end[:, q, :], ident[:])
                    mm.then_inc(blocks_found, 1)
                    pe.wait_ge(ends_ready, 2)
                    for q, banks in enumerate(((0, 1), (4, 7))):
                        for c, bank in enumerate(banks):
                            mm = nc.tensor.matmul(ps[0:1, bank, 0:NT_A // 2], ones[0:NB, 0:1],
                                                  past[:, q, c * (NT_A // 2):(c + 1) * (NT_A // 2)], start=True, stop=True)
                    mm.then_inc(blocks_found, 1)
                chain = ps[:, 6, :].rearrange("p (j c) -> p j c", c=P)[:, :, 0:bins]
                pe.wait_ge(sort_ready, k + 1)
                nc.tensor.matmul(chain, ident[:], base[:, k:k + 1, 0:bins].to_broadcast([P, ST, bins]),
                                 start=True, stop=False, skip_group_check=True)
                with pe.Fori(0, nt // (2 * ST)) as i:
                    for h in range(2):
                        oh = oh_ring[:, h, :, 0:bins]
                        pe.wait_ge(onehot_ready, i * 2 + (g0 + h + 1 + k))
                        for j in range(ST - 1):
                            nc.tensor.matmul(chain[:, j + 1:ST], ones[:], oh[:, j:j + 1].to_broadcast([P, ST - 1 - j, bins]),
                                             start=False, stop=False, skip_group_check=True)
                        nc.tensor.matmul(chain, before[:], oh, start=False, stop=False,
                                         skip_group_check=True).then_inc(prefix_ready, 1)
                        if k == 0:
                            (src_degrees, dst_degrees)[h](i)
                        pe.wait_ge(prefix_read, i * 2 + (g0 + h + 1))
                        for j in range(1, ST):
                            nc.tensor.matmul(chain[:, 0:j], ones[:], oh[:, j:j + 1].to_broadcast([P, j, bins]),
                                             start=False, stop=False, skip_group_check=True)
                        nc.tensor.matmul(chain, not_before[:], oh, start=False, stop=False, skip_group_check=True)

            def to_scan(k, t):
                pe.wait_ge(layout_src, k + 1)
                for c in range(SCAN_C):
                    mm = nc.tensor.transpose(psf[:, 2048 + c * P:2048 + (c + 1) * P], t[:].rearrange("q (p c) -> q c p", c=SCAN_C)[:, c, :], ident[:])
                mm.then_inc(layout_done, 1)

            def to_tiles(k, v):
                pe.wait_ge(layout_src, k + 1)
                for c in range(SCAN_C):
                    mm = nc.tensor.transpose(psf[:, 2048 + c * P:2048 + (c + 1) * P], v[:, c * P:(c + 1) * P], ident[:])
                mm.then_inc(layout_done, 1)

            def carries(k):
                pe.wait_ge(carry_in, 2 * k + 1)
                nc.tensor.transpose(ps[0:1, 6, 0:P], carry_col[:], ident[:]).then_inc(carry_t, 1)
                pe.wait_ge(carry_in, 2 * k + 2)
                nc.tensor.transpose(ps[:, 7, 0:1], row_b[:], ident[0:1, 0:1]).then_inc(carry_t, 1)

            def dense(m, sources):
                pe.wait_ge(dense_src, m + 1)
                for q, (b, n) in enumerate(BATCHES):
                    for s, (rows, w) in enumerate(sources):
                        t = dense_t[m] + q * len(sources) + s
                        if t >= 2:
                            pe.wait_ge(turned_copied, t - 1)
                        for j in range(n):
                            mm = nc.tensor.transpose(ps[:, t % 2, j * P:(j + 1) * P], rows[:, b + j, :], ident[:])
                        mm.then_inc(turned, 1)
                    u = dense_b[m] + q
                    if u >= 2:
                        pe.wait_ge(dense_read, u - 1)
                    for s, (rows, w) in enumerate(sources):
                        t = dense_t[m] + q * len(sources) + s
                        pe.wait_ge(turned_copied, t + 1)
                    for j in range(n):
                        for s, (rows, w) in enumerate(sources):
                            t = dense_t[m] + q * len(sources) + s
                            mm = nc.tensor.matmul(ps[:, 2 + u % 2, j * D:(j + 1) * D], xt_ring[:, t % 2, j * P:(j + 1) * P], w,
                                                  start=(s == 0), stop=(s == len(sources) - 1))
                    mm.then_inc(turned_used, len(sources))

            def aggregate(k):
                kind, _, clears, _ = PASSES[k]
                blk = blk_d if kind[:3] == "dst" else blk_s
                g0 = pass_base[k]
                arrived = landed[k >= LANDED_SPLIT]
                first = (g0 - (pass_base[LANDED_SPLIT] if k >= LANDED_SPLIT else 0)) // 2
                if clears:
                    pe.wait_ge(pass_ready, k + 1)
                    for q in range(7):
                        nc.tensor.matmul(ps[:, q, :], ones[:], zeros[:], start=True, stop=False, skip_group_check=True)
                with pe.Fori(0, (pass_base[k + 1] - g0) // 2) as i:
                    for h in range(2):
                        blocks = [pe.value_load(blk[0:1, bass.ds((i * 2 + h) * GT + j, 1)], min_val=0, max_val=NB - 1)
                                  for j in range(GT)]
                        pe.wait_ge(weights_ready, i * 2 + (g0 + h + 1))
                        pe.wait_ge(arrived[h], i * (16 * GT) + 16 * GT * (first + 1))
                        for j in range(GT):
                            mm = nc.tensor.matmul(acc[:, bass.ds(blocks[j] * D, D)], dw_ring[:, h, j, :], row_ring[:, h, j, :],
                                                  start=False, stop=False, skip_group_check=True)
                        mm.then_inc(tiles_done, 1)

            def scores(l):
                pe.wait_ge(parts_ready, l + 1)
                with pe.Fori(0, SG // 2) as i:
                    for h in range(2):
                        pe.wait_ge(oht_ready, i * 2 + (l * (SG + 1) + h + 3))
                        pe.wait_ge(score_read, i * 2 + (l * SG + h + 1))
                        pg = tiles_bank(h)
                        for j in range(GT):
                            for s, parts in enumerate((hs_parts, hd_parts)):
                                for part in range(3):
                                    mm = nc.tensor.matmul(pg[:, j, s * NB:(s + 1) * NB], oht_ring[:, h, s, j * P:(j + 1) * P],
                                                          parts[:, part, :], start=(part == 0), stop=(part == 2))
                        mm.then_inc(score_mm, 1)

            to_scan(0, t_alpha)
            pe.wait_ge(layout_read, 1)
            to_scan(1, t_srclo)
            pe.wait_ge(layout_read, 2)
            to_scan(2, t_lo)
            for k in range(2):
                pe.wait_ge(carry_in, k + 1)
                nc.tensor.transpose(ps[0:1, 6, 0:P], carry_col[:], ident[:]).then_inc(carry_t, 1)
            pe.sem_inc(tiles_done, 2)
            pe.sem_inc(score_mm, 2)

            pe.wait_ge(weights_loaded, 16 * (1 + NL + 16))
            aggregate(0)
            dense(0, [(AGG, w0[:])])
            aggregate(1)
            dense(1, [(AGG, w_neigh[:, 0]), (H, w_self[:, 0])])
            aggregate(2)
            dense(2, [(AGG, w_neigh[:, 1]), (TA, w_self[:, 1])])
            for k, rows in enumerate((H, TB)):
                pe.wait_ge(bn_src, k + 1)
                for b in range(NB):
                    mm = nc.tensor.matmul(ps[:, 7, 0:D], ones_f[:], rows[:, b, :], start=(b == 0), stop=(b == NB - 1))
                mm.then_inc(bn_sum, 1)
            for k in range(3, 7):
                aggregate(k)
            lay, car = 3, 1
            for l in range(NL):
                src = {0: H}.get(l, AGG)
                dense(m_rows(l), [(src, w_gat[:, l])])
                scores(l)
                to_scan(lay, t_alpha)
                for c in range(4):
                    carries(car + c)
                car += 4
                to_tiles(lay + 1, sc_ex)
                lay += 2
                aggregate(7 + l)
                if 1 <= l <= MID:
                    dense(m_mid(l), [(AGG, w_mid[:, l - 1])])

        @block.vector
        def _(v):
            V = nc.vector
            def bc(t, shape):
                return t.to_broadcast(shape)

            V.memset(blank, 0.0)
            V.memset(zeros[:], 0.0)
            V.memset(ones[:], 1.0)
            V.memset(ones_f[:], 1.0)
            V.memset(guard[:], -2.0)
            V.memset(cnt[:], 0.0)
            V.memset(rec_ring[:], 0.0)
            V.memset(dw_ring[:], 0.0)
            V.memset(oh_shi_t[:], 0.0)
            v.drain()
            V.memset(blank[:, :, F_DST:F_DST + 1], -1.0).then_inc(blank_ready, 1)
            V.memset(recf, 0.0)
            v.drain()
            V.memset(REC[:, :, F_DST:F_DST + 1], -1.0)
            v.wait_ge(iotas, NCONST)
            V.tensor_copy(col_f[:], col_i[:])
            V.tensor_copy(pid_f[:], pid_i[:])
            v.drain()
            V.tensor_scalar(ident[:], col_f[:, 0:P], pid_f[:], None, ALU.is_equal)
            V.tensor_scalar(before_f[:], col_f[:, 0:P], pid_f[:], None, ALU.is_gt)
            V.tensor_scalar(before[:], col_f[:, 0:P], pid_f[:], None, ALU.is_gt)
            V.tensor_scalar(not_before[:], col_f[:, 0:P], pid_f[:], None, ALU.is_le)
            V.tensor_scalar(node_id[:], col_f[:, 0:NB], float(P), pid_f[:], ALU.mult, ALU.add)
            V.tensor_scalar(dump_f[:], pid_f[:], float(DUMP), None, ALU.add)
            v.drain()
            V.tensor_scalar(is_node[:], node_id[:], float(N), None, ALU.is_lt)
            v.wait_ge(weights_loaded, 16 * (1 + NL + 16))
            V.tensor_tensor(aprod, wes, aedge, ALU.mult)
            v.drain()
            V.tensor_reduce(vcol[0:NL * ED, :], aprod, AX_X, ALU.add)
            v.drain()
            V.tensor_copy(base_col[0:NL * ED, :], bc(vcol[0:NL * ED, :], [NL * ED, P])).then_inc(vcol_ready, 1)
            v.wait_ge(vproj_ready, 1)
            V.tensor_copy(vproj[:], ps[:, 7, 0:NL * ED])
            v.wait_ge(edges_loaded, 64)
            for f, view in ((F_SRC, src_i), (F_DST, dst_i), (F_TYPE, type_i), (F_W, w_in)):
                V.tensor_copy(REC[0:EP, 0:EC, f], view)
            V.memset(REC[0:EP, 0:EC, F_VALID:F_VALID + 1], 1.0)
            for vals, lo, hi in ((dst_i, lo_dst, hi_dst), (src_i, lo_src, hi_src)):
                V.tensor_scalar(dig_i, vals, P - 1, None, ALU.bitwise_and)
                v.drain()
                V.tensor_copy(lo, dig_i)
                v.drain()
                V.tensor_scalar(dig_i, vals, 7, None, ALU.arith_shift_right)
                v.drain()
                V.tensor_copy(hi, dig_i)
                v.drain()
            loops = slice(EC, EC + NB)
            V.tensor_copy(REC[:, loops, F_SRC], node_id[:])
            V.tensor_copy(REC[:, loops, F_DST], node_id[:])
            v.drain().then_inc(src_onehots, 1)
            for b, n in BATCHES:
                V.tensor_tensor(src_eq[:, 0:n, :], bc(col_f[0:EP, b:b + n].unsqueeze(2), [EP, n, EC]),
                                bc(hi_src.unsqueeze(1), [EP, n, EC]), ALU.is_equal)
                v.drain()
                V.tensor_reduce(cnt[0:EP, b:b + n], src_eq[:, 0:n, :], AX_X, ALU.add)
                v.drain()

            def tiles_and_base(k, bank, b_i):
                V.tensor_scalar(smallA[:], ps[:, bank, 0:NB], float(P - 1), None, ALU.add)
                v.drain()
                V.tensor_copy(tiles_i[:], smallA[:])
                v.drain()
                V.tensor_scalar(tiles_i[:], tiles_i[:], 7, None, ALU.arith_shift_right)
                v.drain()
                V.tensor_copy(tiles_of[:], tiles_i[:])
                v.drain()
                V.tensor_tensor_scan(tiles_end[:, k, :], ones_f[:, 0:NB], tiles_of[:], 0.0, ALU.mult, ALU.add)
                v.drain()
                V.tensor_tensor(smallB[:], tiles_end[:, k, :], tiles_of[:], ALU.subtract)
                v.drain()
                V.tensor_scalar(base[:, b_i, 0:NB], smallB[:], float(P), None, ALU.mult)

            v.drain().then_inc(counts_ready, 1)
            v.wait_ge(counts_summed, 1)
            tiles_and_base(1, 4, 0)

            def sort_pass(k, beside=None, arrivals=(None,)):
                stretches = len(arrivals)
                nt, bins, _ = SORTS[k]
                turns = nt // (2 * ST) // stretches
                assert turns * stretches * 2 * ST == nt
                io = col_f[:, 0:bins].unsqueeze(1)

                def onehot(h, first):
                    return V.tensor_tensor(oh_ring[:, h, :, 0:bins], bc(io, [P, ST, bins]),
                                           bc(key[:, bass.ds(first, ST)].unsqueeze(2), [P, ST, bins]), ALU.is_equal)

                v.drain()
                onehot(0, 0).then_inc(onehot_ready, 1)
                v.drain().then_inc(sort_ready, 1)
                for stretch in range(stretches):
                    t0 = stretch * turns * 2 * ST
                    g0 = sort_base[k] + t0 // ST
                    if beside:
                        v.wait_ge(arrivals[stretch], 16)
                    with v.Fori(0, turns) as i:
                        for h in range(2):
                            tl = bass.ds(i * 2 * ST + (t0 + h * ST), ST)
                            prod = rank_prod[:, :, 0:bins]
                            v.wait_ge(prefix_ready, i * 2 + (g0 + h + 1))
                            V.tensor_tensor(prod, ps[:, 6, :].rearrange("p (j c) -> p j c", c=P)[:, :, 0:bins],
                                            oh_ring[:, h, :, 0:bins], ALU.mult).then_inc(prefix_read, 1)
                            onehot(1 - h, i * 2 * ST + (t0 + (h + 1) * ST)).then_inc(onehot_ready, 1)
                            V.tensor_scalar(inv[:, h], col_f[:, tl], float(P), dump_f[:], ALU.mult, ALU.add)
                            v.drain()
                            V.tensor_reduce(posf[:, h], prod, AX_X, ALU.add)
                            V.scalar_tensor_tensor(out=inv[:, h], in0=key[:, tl], scalar=0.0, in1=inv[:, h], op0=ALU.is_lt, op1=ALU.mult)
                            v.drain()
                            v.wait_ge(scattered[h], i * (16 * ST) + 16 * ST * (g0 // 2 + 1))
                            V.tensor_tensor(pos_ring[:, h, :], posf[:, h], inv[:, h], ALU.add).then_inc(pos_ready, 1)
                            if beside:
                                beside(stretch, i, h)
                v.wait_ge(prefix_ready, sort_base[k + 1])
                v.drain()

            iota_p = bc(col_f[0:EP, 0:P].unsqueeze(1), [EP, GT, P])
            iota_b = bc(col_f[0:EP, 0:NB].unsqueeze(1), [EP, GT, NB])

            def scores_and_degrees(stretch, i, h):
                c0 = stretch * EA_COLS
                tl = bass.ds(i * GT + c0, GT)
                turn = stretch * (EA_COLS // GT)
                if h == 0:
                    here = ea[stretch][:, bass.ds(i * GT, GT), :]
                    V.tensor_tensor(ea_prod, bc(here.unsqueeze(1), [EP, NL, GT, ED]),
                                    bc(vproj[0:EP].rearrange("p (l k) -> p l k", k=ED).unsqueeze(2), [EP, NL, GT, ED]), ALU.mult)
                    v.wait_ge(dst_multiplied, i + (turn + 1))
                    V.tensor_tensor(oh_dhi[:, :, 0, :], iota_b, bc(hi_dst[:, tl].unsqueeze(2), [EP, GT, NB]), ALU.is_equal)
                    V.tensor_tensor(oh_dlo, iota_p, bc(lo_dst[:, tl].unsqueeze(2), [EP, GT, P]), ALU.is_equal)
                    v.drain()
                    V.tensor_reduce(REC[0:EP, tl, F_C:F_C + NL].rearrange("p t l -> p l t"), ea_prod, AX_X, ALU.add)
                    v.drain()
                    V.tensor_tensor(oh_dhi[:, :, 1:6, :], bc(oh_dhi[:, :, 0:1, :], [EP, GT, NL, NB]),
                                    bc(REC[0:EP, tl, F_C:F_C + NL].unsqueeze(3), [EP, GT, NL, NB]), ALU.mult).then_inc(dst_onehots, 1)
                else:
                    v.wait_ge(src_multiplied, i + (turn + 1))
                    V.tensor_tensor(oh_slo, iota_p, bc(lo_src[:, tl].unsqueeze(2), [EP, GT, P]), ALU.is_equal)
                    V.tensor_tensor(oh_shi, iota_b, bc(hi_src[:, tl].unsqueeze(2), [EP, GT, NB]), ALU.is_equal).then_inc(src_onehots, 1)

            V.memset(key[:], -1.0)
            v.drain()
            V.tensor_copy(key[0:EP, 0:EC], hi_src)
            sort_pass(0, scores_and_degrees, attr_loaded)
            V.memset(X[:, NB - 1, :], 0.0).then_inc(x_cleared, 1)
            v.wait_ge(dst_multiplied, EC // GT + 1)
            v.wait_ge(src_multiplied, EC // GT + 1)
            V.tensor_copy(deg_dst[:], ps[:, 0, 0:NB])
            V.tensor_copy(deg_src[:], ps[:, 1, 0:NB])
            v.drain()
            V.tensor_scalar(rs_dst[:], deg_dst[:], 1.0, None, ALU.max)
            V.tensor_scalar(rs_src[:], deg_src[:], 1.0, None, ALU.max)
            V.tensor_tensor(cnt[:], deg_dst[:], is_node[:], ALU.add)
            v.drain()
            V.tensor_reduce(col1[:], cnt[:], AX_X, ALU.add)
            v.drain().then_inc(counts_ready, 1)
            V.reciprocal(rdeg[:], rs_dst[:])
            v.drain()
            for l in range(NL):
                V.tensor_tensor(REC[:, loops, F_C + l], ps[:, 0, (1 + l) * NB:(2 + l) * NB], rdeg[:], ALU.mult)
            v.wait_ge(counts_summed, 2)
            V.tensor_copy(base_col[:], bc(ps[:, 2, 0:1], [P, P])).then_inc(counts_ready, 1)
            tiles_and_base(0, 3, 2)
            v.drain().then_inc(ends_ready, 1)
            v.wait_ge(counts_summed, 3)
            V.tensor_copy(base[:, 1, :], ps[:, 5, 0:P])
            v.wait_ge(blocks_found, 1)
            for q in range(2):
                V.tensor_copy(ends_col[:, q:q + 1], ps[0:NB, 3, q * P:q * P + 1])
            v.drain()
            for q in range(2):
                V.tensor_scalar(past[:, q, :], col_f[0:NB, :], ends_col[:, q:q + 1], None, ALU.is_ge)
            v.drain().then_inc(ends_ready, 1)
            v.wait_ge(blocks_found, 2)
            for blk, banks in ((blk_d, (0, 1)), (blk_s, (4, 7))):
                for c, bank in enumerate(banks):
                    V.tensor_scalar(blk[:, c * (NT_A // 2):(c + 1) * (NT_A // 2)], ps[0:1, bank, 0:NT_A // 2],
                                    float(NB - 1), None, ALU.min)
            V.memset(key[:], -1.0)
            v.drain()
            V.tensor_copy(key[0:EP, 0:EC], lo_dst)
            V.tensor_scalar(smallA[:], is_node[:], pid_f[:], None, ALU.mult)
            v.drain()
            V.tensor_tensor(smallA[:], smallA[:], is_node[:], ALU.add)
            v.drain()
            V.tensor_scalar(key[:, loops], smallA[:], -1.0, None, ALU.add)
            sort_pass(1)
            v.wait_ge(rec_loaded, 16)
            V.memset(key[:], -1.0)
            hi_i = t_alpha[:, 0:NT_HIGH].bitcast(I32)
            V.tensor_copy(hi_i, REC[:, 0:NT_HIGH, F_DST])
            v.drain()
            V.tensor_scalar(hi_i, hi_i, 7, None, ALU.arith_shift_right)
            v.drain()
            V.tensor_copy(key[:, 0:NT_HIGH], hi_i)
            sort_pass(2)

            v.wait_ge(rec_loaded, 32)
            lo_i = flat(TB)[:, 0:NT_D].bitcast(I32)

            def low_digits(out_t, n, field, pad_field):
                V.tensor_copy(lo_i[:, 0:n], REC[:, 0:n, field])
                v.drain()
                V.tensor_scalar(lo_i[:, 0:n], lo_i[:, 0:n], P - 1, None, ALU.bitwise_and)
                V.tensor_scalar(t_alpha[:, 0:n], REC[:, 0:n, pad_field], 0.0, -float(2 * P), ALU.is_lt, ALU.mult)
                v.drain()
                V.tensor_tensor(out_t, lo_i[:, 0:n], t_alpha[:, 0:n], ALU.add)
                v.drain()

            V.memset(t_lo[:], -1.0)
            V.memset(t_srclo[:], 0.0)
            v.drain()
            low_digits(t_lo[:, 0:NT_D], NT_D, F_DST, F_DST)
            low_digits(t_srclo[:, 0:NT_D], NT_D, F_SRC, F_SRC)
            for s, field in enumerate((F_SRC, F_DST)):
                V.tensor_copy(lo_i, REC[:, :, field])
                v.drain()
                V.tensor_scalar(lo_i, lo_i, 7, None, ALU.arith_shift_right)
                v.drain()
                V.tensor_copy(t_hi[:, :, s], lo_i)
                v.drain()
            V.tensor_copy(t_src[:], REC[:, :, F_SRC])
            V.tensor_copy(t_type[:], REC[:, :, F_TYPE])
            V.tensor_copy(t_w[:], REC[:, :, F_W])
            V.tensor_copy(t_valid[:], REC[:, :, F_VALID])
            v.drain()
            V.memset(t_alpha[:], -1.0)
            for l in range(NL):
                V.tensor_copy(t_c[:, l, :], REC[:, :, F_C + l])
            v.drain()
            V.tensor_copy(t_alpha[:, 0:NT_D], REC[:, :, F_DST])
            v.drain().then_inc(rec_free, 1)
            v.wait_ge(rec_loaded, 48)
            f_dst, f_type, f_lo, f_valid, f_neg = s_found
            V.tensor_scalar(f_dst.bitcast(U32), REC[:, 0:NT_S, F_DST], 0.0, None, ALU.max)
            V.tensor_copy(f_type.bitcast(U32), REC[:, 0:NT_S, F_TYPE])
            V.tensor_copy(f_valid, REC[:, 0:NT_S, F_VALID])
            V.tensor_scalar(f_neg, REC[:, 0:NT_S, F_VALID], -1.0, None, ALU.mult)
            V.tensor_copy(lo_i[:, 0:NT_S], REC[:, 0:NT_S, F_SRC])
            v.drain()
            V.tensor_scalar(lo_i[:, 0:NT_S], lo_i[:, 0:NT_S], P - 1, None, ALU.bitwise_and)
            v.drain()
            V.tensor_copy(f_lo, lo_i[:, 0:NT_S])
            v.drain().then_inc(layout_src, 1)

            psv = psf[:, 2048:2048 + SQ]
            v.wait_ge(layout_done, 1)
            V.tensor_copy(sc_score, psv).then_inc(slot_rows, 1)
            v.drain().then_inc(layout_read, 1)
            for k in range(2):
                v.drain().then_inc(layout_src, 1)
                v.wait_ge(layout_done, 2 + k)
                V.tensor_copy(scan_view(1 + k).bitcast(BF16)[:, 0:SQ], psv).then_inc(slot_rows, 1)
                v.drain().then_inc(layout_read, 1)
            v.wait_ge(neigh_loaded, 32)
            V.tensor_tensor(sc_keepf, sc_score, sc_tot, ALU.is_equal)
            V.tensor_tensor(sc_keepb, sc_score, sc_ex, ALU.is_equal)
            v.drain()
            V.tensor_scalar(sc_neg, sc_keepf, BIG, -BIG, ALU.mult, ALU.add)
            V.tensor_scalar(sc_end, sc_keepb, -1.0, 1.0, ALU.mult, ALU.add)
            for k, keep in enumerate((sc_keepf, sc_keepb)):
                v.drain()
                V.tensor_reduce(carry_col[:], keep, AX_X, ALU.min)
                v.drain().then_inc(carry_in, 1)
                v.wait_ge(carry_t, k + 1)
                V.tensor_copy(keep_rows[:, 1 + k, :], ps[0:1, 6, 0:P])
            v.drain()
            V.tensor_scalar(keep_rows[:, 0, :], keep_rows[:, 1, :], BIG, -BIG, ALU.mult, ALU.add)
            v.wait_ge(slot_stored, 32)
            for found, kept in zip(s_found, s_kept):
                V.tensor_copy(kept.bitcast(I32), found.bitcast(I32))

            def rows3(t, b=NB):
                return bc(t.unsqueeze(1), [P, b, D])

            def cols3(t):
                return bc(t.unsqueeze(2), [P, NB, D])

            def rsqrt_of(root, square, tmp):
                V.reciprocal(root, root)
                v.drain()
                V.tensor_tensor(tmp, root, root, ALU.mult)
                v.drain()
                V.tensor_tensor(tmp, tmp, square, ALU.mult)
                v.drain()
                V.tensor_scalar(tmp, tmp, -0.5, 1.5, ALU.mult, ALU.add)
                v.drain()
                V.tensor_tensor(root, root, tmp, ALU.mult)
                v.drain()

            def norm(k):
                v.drain()
                V.tensor_reduce(smallB[:], X[:], AX_X, ALU.add)
                v.drain()
                V.tensor_scalar(smallB[:], smallB[:], -1.0 / D, None, ALU.mult)
                v.drain()
                V.tensor_tensor(TA[:], X[:], cols3(smallB[:]), ALU.add)
                v.drain()
                V.tensor_tensor(TB[:], TA[:], TA[:], ALU.mult)
                v.drain()
                V.tensor_reduce(smallA[:], TB[:], AX_X, ALU.add)
                v.drain()
                V.tensor_scalar(smallA[:], smallA[:], 1.0 / D, EPS, ALU.mult, ALU.add)
                v.drain()
                V.tensor_copy(smallB[:], smallA[:]).then_inc(var_ready, 1)
                v.wait_ge(std_ready, k + 1)
                rsqrt_of(smallB[:], smallA[:], smallC[:])
                V.scalar_tensor_tensor(out=H[:], in0=TA[:], scalar=0.0, in1=cols3(smallB[:]), op0=ALU.max, op1=ALU.mult)
                v.drain()

            def weigh(k):
                kind, wt, _, _ = PASSES[k]
                lo = t_lo if kind[:3] == "dst" else s_lo
                w = wt_of[(kind[:3], wt)]
                g0 = pass_base[k]
                with v.Fori(0, (pass_base[k + 1] - g0) // 2) as i:
                    for h in range(2):
                        v.wait_ge(tiles_done, i * 2 + (g0 + h + 1))
                        for j in range(GT):
                            tl = bass.ds((i * 2 + h) * GT + j, 1)
                            last = V.tensor_scalar(dw_ring[:, h, j, :], col_f[:, 0:P], lo[:, tl], w[:, tl],
                                                   ALU.is_equal, ALU.mult)
                        last.then_inc(weights_ready, 1)

            def gather_sum(k0, k1):
                v.drain().then_inc(pass_ready, 1)
                for k in range(k0, k1):
                    if k > k0:
                        v.drain().then_inc(pass_ready, 1)
                    weigh(k)
                v.wait_ge(tiles_done, pass_base[k1] + 2)

            acc3 = acc.rearrange("p (b d) -> p b d", d=D)

            def each_product(m, f):
                for q, (b, n) in enumerate(BATCHES):
                    u = dense_b[m] + q
                    v.wait_ge(turned_used, dense_t[m] + (q + 1) * DENSE[m])
                    f(ps[:, 2 + u % 2, 0:n * D].rearrange("p (j d) -> p j d", d=D), slice(b, b + n), n)
                    v.drain().then_inc(dense_read, 1)

            v.wait_ge(x_loaded, 32)
            norm(0)
            v.sem_inc(var_ready, 2)
            v.wait_ge(std_ready, 3)
            V.tensor_scalar(smallA[:], deg_dst[:], 1.0, None, ALU.max)
            V.tensor_scalar(smallB[:], deg_src[:], 1.0, None, ALU.max)
            v.drain()
            rsqrt_of(rs_dst[:], smallA[:], smallC[:])
            rsqrt_of(rs_src[:], smallB[:], smallC[:])
            V.tensor_tensor(AGG[:], H[:], cols3(rs_src[:]), ALU.mult).then_inc(table_rows, 1)
            gather_sum(0, 1)
            V.tensor_tensor(AGG[:], acc3, cols3(rs_dst[:]), ALU.mult)
            v.drain().then_inc(dense_src, 1)

            def gcn(prod, blocks, n):
                V.tensor_tensor(TA[:, blocks, :], prod, rows3(b0[:], n), ALU.add)
                v.drain()
                V.scalar_tensor_tensor(out=X[:, blocks, :], in0=TA[:, blocks, :], scalar=0.0, in1=X[:, blocks, :],
                                       op0=ALU.max, op1=ALU.add)
            each_product(0, gcn)

            norm(3)
            v.drain().then_inc(table_rows, 1)
            gather_sum(1, 2)
            V.tensor_tensor(AGG[:], acc3, cols3(rdeg[:]), ALU.mult)
            v.drain().then_inc(dense_src, 1)

            def sage_relu(prod, blocks, n):
                V.tensor_tensor(TA[:, blocks, :], prod, rows3(b1[:, 0], n), ALU.add)
                v.drain()
                V.tensor_scalar(TA[:, blocks, :], TA[:, blocks, :], 0.0, None, ALU.max)
            each_product(1, sage_relu)
            v.drain().then_inc(table_rows, 1)
            gather_sum(2, 3)
            V.tensor_tensor(AGG[:], acc3, cols3(rdeg[:]), ALU.mult)
            v.drain().then_inc(dense_src, 1)

            def sage_gate(prod, blocks, n):
                V.tensor_tensor(TB[:, blocks, :], prod, rows3(b1[:, 1], n), ALU.add)
            each_product(2, sage_gate)
            V.tensor_scalar(TA[:], TB[:], -80.0, None, ALU.max).then_inc(gate_in, 1)
            v.wait_ge(gate_out, 1)
            V.tensor_scalar(TA[:], TA[:], 1.0, None, ALU.add)
            v.drain()
            V.reciprocal(TA[:], TA[:])
            v.drain()
            V.tensor_tensor(X[:], X[:], TA[:], ALU.add)

            norm(4)
            V.tensor_tensor(H[:], H[:], cols3(is_node[:]), ALU.mult)
            v.drain().then_inc(bn_src, 1)
            v.wait_ge(bn_sum, 1)
            V.tensor_scalar(bn_row[:], ps[:, 7, 0:D], -1.0 / N, None, ALU.mult)
            v.drain()
            V.tensor_tensor(TA[:], H[:], rows3(bn_row[:]), ALU.add)
            v.drain()
            V.tensor_tensor(TA[:], TA[:], cols3(is_node[:]), ALU.mult)
            v.drain()
            V.tensor_tensor(TB[:], TA[:], TA[:], ALU.mult)
            v.drain().then_inc(bn_src, 1)
            v.wait_ge(bn_sum, 2)
            V.tensor_scalar(b0[:], ps[:, 7, 0:D], 1.0 / N, EPS, ALU.mult, ALU.add)
            v.drain()
            V.tensor_copy(bn_row[:], b0[:]).then_inc(var_ready, 1)
            v.wait_ge(std_ready, 6)
            rsqrt_of(bn_row[:], b0[:], bn_tmp[:])
            V.tensor_tensor(bn_row[:], bn_row[:], gamma[:], ALU.mult)
            v.drain()
            V.tensor_tensor(TA[:], TA[:], rows3(bn_row[:]), ALU.mult)
            v.drain()
            V.tensor_tensor(TA[:], TA[:], rows3(beta[:]), ALU.add)
            v.drain()
            V.tensor_tensor(H[:], TA[:], rows3(kern[:]), ALU.mult)
            v.wait_ge(rel_loaded, 16)
            V.tensor_tensor(relr, relr, bc(kern[0:EP].unsqueeze(1), [EP, R // EP, D]), ALU.mult).then_inc(rel_rows, 1)
            v.drain().then_inc(table_rows, 1)
            V.tensor_copy(firsts[:], firsts_i[:])
            V.memset(cnt[:], 1.0)
            for k in range(3):
                v.drain()
                V.tensor_tensor(col1[:], firsts[:, k, 0:1], firsts[:, k, 2:3], ALU.not_equal)
                for e in (0, 2):
                    v.drain()
                    V.tensor_scalar(smallA[:], node_id[:], firsts[:, k, e:e + 1], col1[:], ALU.is_equal, ALU.mult)
                    v.drain()
                    V.tensor_tensor(cnt[:], cnt[:], smallA[:], ALU.add)
            v.drain()
            V.reciprocal(cnt[:], cnt[:])
            gather_sum(3, 7)
            V.tensor_tensor(AGG[:], acc3, H[:], ALU.add)
            v.drain()
            V.tensor_tensor(AGG[:], AGG[:], cols3(cnt[:]), ALU.mult)
            v.drain()
            V.tensor_tensor(X[:], X[:], AGG[:], ALU.add)

            norm(6)
            v.drain().then_inc(dense_src, 1)
            v.sem_inc(score_read, 2)
            v.sem_inc(oht_ready, 2)

            def take_rows(prod, blocks, n):
                V.tensor_copy(TA[:, blocks, :], prod)

            def split(parts, hs):
                V.tensor_copy(parts[:, 0, :], hs)
                for q in (0, 1):
                    v.drain()
                    V.tensor_tensor(hs, hs, parts[:, q, :], ALU.subtract)
                    v.drain()
                    V.tensor_copy(parts[:, q + 1, :], hs)

            def carry(k, keep_row, col, op0, op1, start, back):
                V.tensor_copy(carry_col[:], col)
                v.drain().then_inc(carry_in, 1)
                v.wait_ge(carry_t, 2 * k + 1)
                V.tensor_copy(row_a[:], ps[0:1, 6, 0:P])
                V.memset(carry_row[:], start)
                v.drain()
                r = slice(None, None, -1) if back else slice(None)
                V.tensor_tensor_scan(carry_row[:, 1:P + 1][:, r], keep_row[:, r], row_a[:, r], start, op0, op1)
                v.drain()
                V.tensor_copy(row_b[:], carry_row[:, 2:P + 2] if back else carry_row[:, 0:P])
                v.drain().then_inc(carry_in, 1)
                v.wait_ge(carry_t, 2 * k + 2)
                V.tensor_copy(carry_col[:], ps[:, 7, 0:1])
                v.drain()

            def segment_total(k, data, op0, op1, d0, keep_row, start):
                V.tensor_tensor_scan(sc_fwd, d0, data, start, op0, op1)
                v.drain()
                carry(k, keep_row, sc_fwd[:, SQ - 1:SQ], op0, op1, start, False)
                V.tensor_tensor_scan(sc_fwd, d0, data, carry_col[:], op0, op1)
                v.drain()
                V.tensor_tensor(sc_ends, sc_fwd, sc_end, ALU.mult)
                v.drain()
                V.tensor_tensor_scan(sc_tot[:, ::-1], sc_keepb[:, ::-1], sc_ends[:, ::-1], 0.0, ALU.mult, ALU.add)
                v.drain()
                carry(k + 1, keep_rows[:, 2, :], sc_tot[:, 0:1], ALU.mult, ALU.add, 0.0, True)
                V.tensor_tensor_scan(sc_tot[:, ::-1], sc_keepb[:, ::-1], sc_ends[:, ::-1], carry_col[:], ALU.mult, ALU.add)
                v.drain()

            lay, car = 3, 1
            for l in range(NL):
                each_product(m_rows(l), take_rows)
                v.drain().then_inc(table_rows, 1)
                for av, small, parts in ((a_src, smallA, hs_parts), (a_dst, smallB, hd_parts)):
                    V.tensor_tensor(TB[:], TA[:], rows3(av[:, l]), ALU.mult)
                    v.drain()
                    V.tensor_reduce(small[:], TB[:], AX_X, ALU.add)
                    v.drain()
                    split(parts, small[:])
                v.drain().then_inc(parts_ready, 1)
                n0 = l * SG

                def turn(h, landed_at):
                    v.wait_ge(lo_landed[h], landed_at)
                    return V.tensor_scalar(oht_ring[:, h], lo_ring[:, h], pid_f[:], None, ALU.is_equal)

                half0, half1 = SG // 2 + 1, SG // 2
                v.wait_ge(score_mm, n0 + 1)
                turn(0, 32 * (l * half0 + 1)).then_inc(oht_ready, 1)
                with v.Fori(0, SG // 2) as i:
                    for h in range(2):
                        g = i * 2 + h
                        tl = bass.ds(g * GT, GT)
                        v.wait_ge(score_mm, g + (n0 + 2))
                        if h == 0:
                            turn(1, i * 32 + 32 * (l * half1 + 1)).then_inc(oht_ready, 1)
                        else:
                            turn(0, i * 32 + 32 * (l * half0 + 2)).then_inc(oht_ready, 1)
                        V.tensor_tensor(oh_hi, bc(col_f[:, 0:NB].unsqueeze(1).unsqueeze(1), [P, GT, 2, NB]),
                                        bc(t_hi[:, tl, :].unsqueeze(3), [P, GT, 2, NB]), ALU.is_equal)
                        v.drain()
                        v.wait_ge(score_mm, g + (n0 + 3))
                        V.tensor_tensor(pr_hi, tiles_bank(h)[:, :, 0:2 * NB], oh_hi.rearrange("p t s c -> p t (s c)"),
                                        ALU.mult).then_inc(score_read, 1)
                        v.drain()
                        V.tensor_reduce(t_alpha[:, tl], pr_hi, AX_X, ALU.add)
                v.drain()
                V.memset(t_alpha[:, NT_D:NT_A], 0.0)
                V.tensor_tensor(t_alpha[:, 0:NT_D], t_alpha[:, 0:NT_D], t_c[:, l, :], ALU.add)
                v.drain()
                V.scalar_tensor_tensor(out=t_alpha[:], in0=t_alpha[:], scalar=ATT_SLOPE, in1=t_alpha[:], op0=ALU.mult, op1=ALU.max)
                v.drain().then_inc(layout_src, 1)
                v.wait_ge(layout_done, lay + 1)
                V.tensor_copy(sc_score, psv)
                v.drain()
                segment_total(car, sc_score, ALU.add, ALU.max, sc_neg, keep_rows[:, 0, :], -BIG)
                V.tensor_tensor(sc_ex, sc_score, sc_tot, ALU.subtract).then_inc(exp_in, 1)
                v.wait_ge(exp_out, l + 1)
                segment_total(car + 2, sc_ex, ALU.mult, ALU.add, sc_keepf, keep_rows[:, 1, :], 0.0)
                V.reciprocal(sc_tot, sc_tot)
                v.drain()
                V.tensor_tensor(sc_ex, sc_ex, sc_tot, ALU.mult)
                v.drain().then_inc(layout_src, 1)
                v.wait_ge(layout_done, lay + 2)
                V.tensor_copy(t_alpha[:].rearrange("q (p c) -> q c p", c=SCAN_C), psv.rearrange("q (c p) -> q c p", c=SCAN_C))
                lay, car = lay + 2, car + 4
                gather_sum(7 + l, 8 + l)
                V.tensor_tensor(AGG[:], acc3, rows3(b3[:, l]), ALU.add)
                v.drain()
                if l == 0:
                    V.tensor_copy(X0[:], AGG[:])
                    v.drain().then_inc(dense_src, 1)
                elif l <= MID:
                    keep = math.log(THETA / l + 1.0)
                    V.tensor_scalar(AGG[:], AGG[:], 1.0 - ALPHA, None, ALU.mult)
                    v.drain()
                    V.scalar_tensor_tensor(out=AGG[:], in0=X0[:], scalar=ALPHA, in1=AGG[:], op0=ALU.mult, op1=ALU.add)
                    v.drain().then_inc(dense_src, 1)

                    def mid(prod, blocks, n):
                        V.tensor_scalar(TA[:, blocks, :], prod, keep, None, ALU.mult)
                        v.drain()
                        V.scalar_tensor_tensor(out=TA[:, blocks, :], in0=AGG[:, blocks, :], scalar=1.0 - keep,
                                               in1=TA[:, blocks, :], op0=ALU.mult, op1=ALU.add)
                    each_product(m_mid(l), mid)
                    V.scalar_tensor_tensor(out=AGG[:], in0=TA[:], scalar=OUT_SLOPE, in1=TA[:], op0=ALU.mult, op1=ALU.max)
                    v.drain().then_inc(dense_src, 1)
                else:
                    V.tensor_tensor(X[:], X[:], AGG[:], ALU.add)
            v.drain().then_inc(final_rows, 1)


_INS = ["x", "src", "dst", "edge_attr_16", "edge_type_1000", "edge_weight", "L0_gnn_W", "L0_gnn_b", "L1_gnn_W_self",
        "L1_gnn_W_neigh", "L1_gnn_bias", "L2_gnn_r", "L2_gnn_gamma", "L2_gnn_beta", "L2_gnn_kernels", "L3_gnn_Ws",
        "L3_gnn_Wes", "L3_gnn_a_srcs", "L3_gnn_a_dsts", "L3_gnn_a_edges", "L3_gnn_biases", "L3_gnn_mid_ws"]


def kernel(**inputs):
    import concourse.bacc as _bacc
    from concourse.bass_utils import run_bass_kernel_spmd as _run

    nc = _bacc.Bacc("TRN2", target_bir_lowering=False, num_devices=1)
    arrays, args = {}, {}
    for name in _INS:
        arr = np.ascontiguousarray(inputs[name])
        arrays[f"in_{name}"] = arr
        args[name] = nc.dram_tensor(f"in_{name}", arr.shape, mybir.dt.from_np(arr.dtype), kind="ExternalInput").ap()
    out = nc.dram_tensor("out_x", inputs["x"].shape, F32, kind="ExternalOutput").ap()
    build(nc, args, out)
    r = _run(nc, [arrays], core_ids=[0])
    return r.results[0]["out_x"]
```

```python
from contextlib import ExitStack
import math

import numpy as np
import concourse.bass as bass
from concourse import mybir

F32, I32, U32, BF16 = mybir.dt.float32, mybir.dt.int32, mybir.dt.uint32, mybir.dt.bfloat16
ALU = mybir.AluOpType
ACT = mybir.ActivationFunctionType
AX_X = mybir.AxisListType.X

P = 128
D = 128
BIG = 1e38
RW = 12
F_SRC, F_DST, F_TYPE, F_W, F_VALID, F_C = 0, 1, 2, 3, 4, 5
GT = 8
RR = 4
LR = 4
PACK = 4
ST = 4
SCAN_C = 7
ALPHA, THETA, ATT_SLOPE, OUT_SLOPE, EPS = 0.2, 0.2, 0.2, 0.01, 1e-5


def ceil_to(x, m):
    return -(-x // m) * m


def build(nc, a, out):
    x_in, W0 = a["x"], a["L0_gnn_W"]
    N = x_in.shape[0]
    E = a["src"].shape[0]
    ED = a["edge_attr_16"].shape[1]
    R = a["L2_gnn_r"].shape[0]
    NL = a["L3_gnn_Ws"].shape[0]
    MID = a["L3_gnn_mid_ws"].shape[0]
    NB = -(-N // P)
    TAIL = N - (NB - 1) * P
    EP = 125
    EC = E // EP
    assert EP * EC == E and EC % (2 * ST) == 0 and EC % GT == 0 and R % EP == 0
    EA_CHUNKS = 4
    EA_COLS = EC // EA_CHUNKS
    assert EA_COLS * EA_CHUNKS == EC and EA_COLS % (2 * ST) == 0 and GT == 2 * ST
    ITEMS = E + N
    NT_LOW = ceil_to(EC + NB, 2 * ST)
    NT_HIGH = ceil_to(-(-ITEMS // P), 2 * ST)
    NT_D = ceil_to((ITEMS + NB * (P - 1)) // P, 2 * GT)
    NT_S = ceil_to((E + NB * (P - 1)) // P, 2 * GT)
    NT_A = P * SCAN_C
    assert NB <= 31 and NT_A % PACK == 0 and NT_D + GT <= NT_A and NT_S <= NT_D and NT_HIGH <= NT_D and NT_LOW <= NT_D
    DUMP = NT_D * P
    SPARE = 2 * DUMP
    ROWS = SPARE + 2 * ST
    BLANKS = 8
    BLANK_T = NT_D // BLANKS
    assert BLANK_T * BLANKS == NT_D
    SQ = SCAN_C * P
    BATCHES = [(b, min(4, NB - b)) for b in range(0, NB, 4)]
    NBT = len(BATCHES)

    def scratch(name, shape, dt):
        return nc.dram_tensor(name, shape, dt, kind="Internal").ap()

    rec_low = scratch("rec_low", (ROWS, RW), F32)
    rec_dst = scratch("rec_dst", (ROWS, RW), F32)
    rec_src = scratch("rec_src", (ROWS, RW), F32)
    table = scratch("table", (NB * P, D), F32)
    table_r = scratch("table_r", (R, D), F32)
    lo_d = scratch("lo_d", (P * SQ * 2,), BF16)
    dst_d = scratch("dst_d", (P * SQ + 2,), F32)

    SORTS = [(EC, NB, rec_src), (NT_LOW, P, rec_low), (NT_HIGH, NB, rec_dst)]
    sort_base = [0]
    for nt, _, _ in SORTS:
        sort_base.append(sort_base[-1] + nt // ST)
    PASSES = [("dst", "valid", True, True), ("dst", "w", True, True), ("dst", "w", True, True),
              ("dst_rel", "valid", True, False), ("dst", "valid", False, False),
              ("src_rel", "neg", False, False), ("src", "valid", False, True)]
    PASSES += [("dst", "alpha", True, True)] * NL
    pass_base = [0]
    for kind, _, _, _ in PASSES:
        pass_base.append(pass_base[-1] + (NT_D if kind[:3] == "dst" else NT_S) // GT)
    DENSE = [1, 2, 2] + [1] * (NL + MID)
    dense_t, dense_b = [0], [0]
    for n in DENSE:
        dense_t.append(dense_t[-1] + n * NBT)
        dense_b.append(dense_b[-1] + NBT)

    def m_rows(l):
        return 3 if l == 0 else 2 + 2 * l

    def m_mid(l):
        return 3 + 2 * l

    SG = NT_D // GT
    UN = 2 * LR
    assert SG % UN == 0

    with ExitStack() as ctx:
        def sb(name, shape, dt=F32):
            return ctx.enter_context(nc.sbuf_tensor(name, shape, dt))

        def sem(name):
            return ctx.enter_context(nc.semaphore(name))

        ps = ctx.enter_context(nc.psum_tensor("ps", [P, 8, 512], F32))
        psf = ps[:].rearrange("p b c -> p (b c)")
        acc = psf[:, 0:NB * D]
        W_SUM = 6 * 512 + 256
        assert 6 * 512 < NB * D <= W_SUM and W_SUM + 32 <= 7 * 512

        X = sb("X", [P, NB, D])
        H = sb("H", [P, NB, D])
        AGG = sb("AGG", [P, NB, D])
        TA = sb("TA", [P, NB, D])
        TB = sb("TB", [P, NB, D])
        REC = sb("REC", [P, NT_D, RW])
        X0 = H

        pid_i = sb("pid_i", [P, 1], I32)
        col_f = sb("col_f", [P, NT_A])
        pid_f = sb("pid_f", [P, 1])
        dump_f = sb("dump_f", [P, 1])
        ident = sb("ident", [P, P])
        before_f = sb("before_f", [P, P])
        ones_f = sb("ones_f", [P, P])
        before = sb("before", [P, P], BF16)
        not_before = sb("not_before", [P, P], BF16)
        ones = sb("ones", [P, P], BF16)
        zeros = sb("zeros", [P, 512], BF16)
        node_id = sb("node_id", [P, NB])
        is_node = sb("is_node", [P, NB])
        block_b = sb("block_b", [P, NB], BF16)
        w_att = sb("w_att", [P, NL, 2])
        b3_mix = sb("b3_mix", [P, NL, D])
        guard = sb("guard", [1, 1])

        w0 = sb("w0", [P, D])
        w_self = sb("w_self", [P, 2, D])
        w_neigh = sb("w_neigh", [P, 2, D])
        w_gat = sb("w_gat", [P, NL, D])
        w_mid = sb("w_mid", [P, MID, D])
        b0 = sb("b0", [P, D])
        b1 = sb("b1", [P, 2, D])
        gamma = sb("gamma", [P, D])
        beta = sb("beta", [P, D])
        kern = sb("kern", [P, D])
        a_src = sb("a_src", [P, NL, D])
        a_dst = sb("a_dst", [P, NL, D])
        b3 = sb("b3", [P, NL, D])
        firsts_i = sb("firsts_i", [P, 3, 3], I32)
        firsts = sb("firsts", [P, 3, 3])

        deg_dst = sb("deg_dst", [P, NB])
        deg_src = sb("deg_src", [P, NB])
        rdeg = sb("rdeg", [P, NB])
        rs_dst = sb("rs_dst", [P, NB])
        rs_src = sb("rs_src", [P, NB])
        cnt = sb("cnt", [P, NB])
        col1 = sb("col1", [P, 1])
        base_col = sb("base_col", [P, P])
        base = sb("base", [P, 3, P])
        tiles_of = sb("tiles_of", [P, NB])
        tiles_i = sb("tiles_i", [P, NB], I32)
        tiles_end = sb("tiles_end", [P, 2, NB])
        blk_d = sb("blk_d", [1, NT_A // PACK], I32)
        blk_s = sb("blk_s", [1, NT_A // PACK], I32)
        smallA = sb("smallA", [P, NB])
        smallB = sb("smallB", [P, NB])
        smallC = sb("smallC", [P, NB])
        bn_tmp = sb("bn_tmp", [P, D])
        vcol = sb("vcol", [P, 1])
        vproj = sb("vproj", [P, NL * ED])
        posf = sb("posf", [P, 2, ST])
        inv = sb("inv", [P, 2, ST])
        pos_ring = sb("pos_ring", [P, 2, ST], U32)
        rec_ring = sb("rec_ring", [P, 2, ST, RW])
        oh_ring = sb("oh_ring", [P, 2, ST, P], BF16)

        oh_shi_t = sb("oh_shi_t", [P, GT, NB], BF16)
        ends_col = sb("ends_col", [NB, 3])
        hd_turned = sb("hd_turned", [NB, P])
        bn_row = sb("bn_row", [P, D])

        t_src = sb("t_src", [P, NT_D], U32)
        t_type = sb("t_type", [P, NT_D], U32)
        t_lo = sb("t_lo", [P, NT_A])
        t_w = sb("t_w", [P, NT_D])
        t_valid = sb("t_valid", [P, NT_D])
        t_c = sb("t_c", [P, NL, NT_D])
        t_hi = sb("t_hi", [P, NT_D + GT], BF16)
        t_alpha = sb("t_alpha", [P, NT_A])

        idx_ring = sb("idx_ring", [P, RR, GT], U32)
        row_ring = sb("row_ring", [P, 2, GT, D])
        dw_ring = sb("dw_ring", [P, 2, GT, P])
        xt_ring = sb("xt_ring", [P, 2, 512])
        carry_row = sb("carry_row", [1, P + 2])
        row_a = sb("row_a", [1, P])
        row_b = sb("row_b", [1, P])
        carry_col = sb("carry_col", [P, 1])
        keep_rows = sb("keep_rows", [1, 3, P])
        hs_parts = sb("hs_parts", [P, 3, NB], BF16)
        hd_ring = sb("hd_ring", [P, 2, 3, GT], BF16)
        tile_block = sb("tile_block", [NB, NT_A], BF16)

        recf = REC[:].rearrange("p t w -> p (t w)")
        def scan_view(i):
            return recf[:, i * SQ:(i + 1) * SQ]
        sc_score, sc_fwd, sc_ends, sc_tot, sc_ex = (scan_view(i) for i in range(5))
        sc_neg, sc_keepf, sc_keepb, sc_end = (scan_view(i) for i in range(5, 9))
        assert 9 * SQ + 3 * NT_A // 2 + 3 * P // 2 <= NT_D * RW
        hd_tiles = recf[:, 9 * SQ:9 * SQ + 3 * NT_A // 2].bitcast(BF16).rearrange("p (k t) -> p k t", t=NT_A)
        hd_parts = recf[0:NB, 9 * SQ + 3 * NT_A // 2:9 * SQ + 3 * NT_A // 2 + 3 * P // 2].bitcast(BF16).rearrange(
            "b (k p) -> b k p", p=P)
        flat = lambda t: t[:].rearrange("p b d -> p (b d)")
        s_found = [flat(TA)[:, i * NT_D:i * NT_D + NT_S] for i in range(3)] + [
            flat(TB)[:, i * NT_D:i * NT_D + NT_S] for i in (1, 2)]
        s_kept = [scan_view(i)[:, 0:NT_S] for i in range(5)]
        s_dst, s_type = (t.bitcast(U32) for t in s_kept[0:2])
        s_lo, s_valid, s_neg = s_kept[2:5]
        key = flat(TA)[:, 0:NT_D + 2 * ST]
        t_srclo = flat(H)[:, 2048:2048 + NT_A]
        blk_row = flat(TB)[0:1, 1024:1024 + NT_A]
        blk_pack = flat(TB)[0:1, 1024 + NT_A:1024 + NT_A + NT_A // PACK]
        past = flat(TB)[0:NB, 2304:2304 + NT_A].bitcast(BF16).rearrange("b (s t) -> b s t", t=NT_A)
        col_i = flat(TB)[:, 0:NT_A].bitcast(I32)
        src_i = flat(TA)[0:EP, 0:EC].bitcast(I32)
        dst_i = flat(TA)[0:EP, EC:2 * EC].bitcast(I32)
        type_i = flat(TA)[0:EP, 2 * EC:3 * EC].bitcast(I32)
        w_in = flat(TA)[0:EP, 3 * EC:4 * EC]
        assert 3 * NT_D <= NB * D and 2048 + NT_A <= NB * D and 2304 + NT_A <= NB * D
        assert 4 * EC <= NB * D and EA_COLS * ED <= min(NB * D, NL * NT_D)
        ea = [t[0:EP, 0:EA_COLS * ED].rearrange("p (t k) -> p t k", k=ED)
              for t in (flat(H), t_c[:].rearrange("p l t -> p (l t)"), flat(X), flat(AGG))]
        ea_prod = flat(TB)[0:EP, 1024:1024 + NL * GT * ED].rearrange("p (l t k) -> p l t k", l=NL, k=ED)
        src_eq = flat(TB)[0:EP, 0:4 * EC].rearrange("p (b t) -> p b t", t=EC)
        blank = flat(AGG)[:, 0:BLANK_T * RW].rearrange("p (t w) -> p t w", w=RW)
        wes = flat(AGG)[0:NL * ED, 1600:1600 + D]
        aedge = flat(AGG)[0:NL * ED, 1600 + D:1600 + 2 * D]
        aprod = flat(AGG)[0:NL * ED, 1600 + 2 * D:1600 + 3 * D]
        lo_dst, hi_dst, lo_src, hi_src = (t[0:EP, 0:EC] for t in (t_lo, t_type[:].bitcast(F32), t_w, t_valid))
        dig_i = t_alpha[0:EP, 0:EC].bitcast(I32)
        oh_dlo = dw_ring[0:EP, 0]
        oh_slo = dw_ring[0:EP, 1].rearrange("p a b -> p (a b)").bitcast(BF16)[:, 0:GT * P].rearrange("p (t c) -> p t c", c=P)
        oh_dhi = row_ring[0:EP].rearrange("p a b d -> p (a b d)")[:, 0:GT * 6 * NB].rearrange(
            "p (t l c) -> p t l c", l=6, c=NB)
        oh_shi = oh_shi_t[0:EP]
        relr = row_ring[0:EP].rearrange("p a b d -> p (a b) d")[:, 0:R // EP, :]
        rank_prod = TB[:, 0:ST, :]
        agg_rows = flat(AGG)[:, 0:2 * GT * D].rearrange("p (h j d) -> p h j d", h=2, d=D)
        rows_in = [row_ring[:, 0], row_ring[:, 1], agg_rows[:, 0], agg_rows[:, 1]]
        lo_ring = [t[:, o:o + GT * P].bitcast(BF16) for t, o in
                   ((flat(TB), 1024), (flat(TB), 1024 + GT * P), (flat(TA), 0), (flat(TA), GT * P))]
        oht_flat = dw_ring[:].rearrange("p a b d -> p (a b d)").bitcast(BF16).rearrange("p (h c) -> p h c", h=2)
        oht_ring = oht_flat.rearrange("p h (t s c) -> p h t s c", t=GT, s=2)
        oh_hi = flat(TB)[:, 0:2 * GT * NB].rearrange("p (h t c) -> p h t c", h=2, c=NB)
        pr_hi = flat(TB)[:, 512:512 + 2 * GT * NB].rearrange("p (h t c) -> p h t c", h=2, c=NB)
        assert 2 * GT * NB <= 512 and 1024 + 2 * GT * P <= NB * D and 2 * GT <= NB

        idx_of = {"dst": t_src, "dst_rel": t_type, "src": s_dst, "src_rel": s_type}
        wt_of = {("dst", "valid"): t_valid, ("dst", "w"): t_w, ("dst", "alpha"): t_alpha,
                 ("src", "valid"): s_valid, ("src", "neg"): s_neg}

        def tiles_bank(t):
            return psf[:, t * 1024:(t + 1) * 1024].rearrange("p (j c) -> p j c", c=P)

        iotas = sem("iotas")
        consts_ready = sem("consts_ready")
        x_cleared = sem("x_cleared")
        x_loaded = sem("x_loaded")
        edges_loaded = sem("edges_loaded")
        weights_loaded = sem("weights_loaded")
        blank_ready = sem("blank_ready")
        blanked = sem("blanked")
        attr_loaded = [sem(f"attr_loaded{i}") for i in range(EA_CHUNKS)]
        vcol_ready = sem("vcol_ready")
        vproj_ready = sem("vproj_ready")
        dst_onehots = sem("dst_onehots")
        src_onehots = sem("src_onehots")
        dst_multiplied = sem("dst_multiplied")
        src_multiplied = sem("src_multiplied")
        ends_ready = sem("ends_ready")
        blocks_found = sem("blocks_found")
        counts_ready = sem("counts_ready")
        counts_summed = sem("counts_summed")
        sort_ready = sem("sort_ready")
        onehot_ready = sem("onehot_ready")
        prefix_ready = sem("prefix_ready")
        prefix_read = sem("prefix_read")
        pos_ready = sem("pos_ready")
        rec_staged = sem("rec_staged")
        scattered = [sem(f"scattered{i}") for i in range(2)]
        rec_loaded = sem("rec_loaded")
        rec_free = sem("rec_free")
        slots_ready = sem("slots_ready")
        layout_src = sem("layout_src")
        layout_done = sem("layout_done")
        layout_read = sem("layout_read")
        slot_rows = sem("slot_rows")
        slot_stored = sem("slot_stored")
        dst_stored = sem("dst_stored")
        neigh_loaded = sem("neigh_loaded")
        var_ready = sem("var_ready")
        std_ready = sem("std_ready")
        table_rows = sem("table_rows")
        table_written = sem("table_written")
        rel_loaded = sem("rel_loaded")
        rel_rows = sem("rel_rows")
        idx_staged = sem("idx_staged")
        landed = [sem(f"landed{i}") for i in range(RR)]
        weights_ready = sem("weights_ready")
        tiles_done = sem("tiles_done")
        pass_ready = sem("pass_ready")
        dense_src = sem("dense_src")
        turned = sem("turned")
        turned_copied = sem("turned_copied")
        turned_used = sem("turned_used")
        dense_read = sem("dense_read")
        gate_in = sem("gate_in")
        gate_out = sem("gate_out")
        bn_src = sem("bn_src")
        bn_sum = sem("bn_sum")
        parts_ready = sem("parts_ready")
        hd_in = sem("hd_in")
        hd_out = sem("hd_out")
        hd_staged = sem("hd_staged")
        lo_landed = [sem(f"lo_landed{i}") for i in range(LR)]
        oht_ready = sem("oht_ready")
        score_mm = sem("score_mm")
        score_read = sem("score_read")
        carry_in = sem("carry_in")
        carry_t = sem("carry_t")
        exp_in = sem("exp_in")
        exp_out = sem("exp_out")
        final_rows = sem("final_rows")
        out_written = sem("out_written")

        def tile_blocks(eng, blk, word):
            words = [eng.value_load(blk[0:1, bass.ds(word + q, 1)], min_val=0, max_val=32 ** PACK - 1) for q in range(GT // PACK)]
            return [(words[j // PACK] >> (5 * (j % PACK))) & 31 for j in range(GT)]

        def each_group(eng, k, f):
            n = pass_base[k + 1] - pass_base[k]
            with eng.Fori(0, n // RR) as i:
                for u in range(RR):
                    f(i, u)
            for u in range(n // RR * RR, n):
                f(0, u)

        NCONST = 2
        block = ctx.enter_context(nc.Block())

        @block.sync
        def _(sp):
            for view, name in ((src_i, "src"), (dst_i, "dst"), (type_i, "edge_type_1000"), (w_in, "edge_weight")):
                sp.dma_start(view, a[name].rearrange("(p t) -> p t", p=EP)).then_inc(edges_loaded, 16)
            sp.dma_start(wes, a["L3_gnn_Wes"].rearrange("l k d -> (l k) d")).then_inc(weights_loaded, 16)
            for l in range(NL):
                sp.dma_start(aedge[l * ED:(l + 1) * ED, :],
                             a["L3_gnn_a_edges"][l, :].partition_broadcast(ED)).then_inc(weights_loaded, 16)
            attr = a["edge_attr_16"].rearrange("(p t) k -> p t k", p=EP)
            for i in range(EA_CHUNKS):
                if i == EA_CHUNKS - 1:
                    sp.wait_ge(vcol_ready, 1)
                    sp.wait_ge(blanked, 16 * 3 * BLANKS)
                    for h in range(2):
                        sp.wait_ge(scattered[h], 16 * ST)
                sp.dma_start(ea[i], attr[:, i * EA_COLS:(i + 1) * EA_COLS, :]).then_inc(attr_loaded[i], 16)
            sp.wait_ge(x_cleared, 1)
            sp.dma_start(X[:, 0:NB - 1, :], x_in[0:(NB - 1) * P, :].rearrange("(b p) f -> p b f", p=P)).then_inc(x_loaded, 16)
            sp.dma_start(X[0:TAIL, NB - 1, :], x_in[(NB - 1) * P:N, :]).then_inc(x_loaded, 16)
            sp.dma_start(relr, a["L2_gnn_r"].rearrange("(p t) d -> p t d", p=EP)).then_inc(rel_loaded, 16)
            sp.wait_ge(rel_rows, 1)
            sp.dma_start(table_r.rearrange("(p t) d -> p t d", p=EP), relr).then_inc(table_written, 16)

            def store_table(k, rows):
                sp.wait_ge(table_rows, k + 1)
                sp.dma_start(table.rearrange("(b p) f -> p b f", p=P), rows[:, :, :]).then_inc(table_written, 16)

            n = sort_base[2] // 2
            for h in range(2):
                sp.wait_ge(scattered[h], 16 * ST * (n + 1))
            sp.dma_start(REC[:, 0:NT_HIGH, :],
                         rec_low[0:NT_HIGH * P, :].rearrange("(t q) w -> q t w", q=P)).then_inc(rec_loaded, 16)
            n = sort_base[3] // 2
            for h in range(2):
                sp.wait_ge(scattered[h], 16 * ST * (n + 1))
            sp.dma_start(REC[:, 0:NT_D, :],
                         rec_dst[0:NT_D * P, :].rearrange("(t q) w -> q t w", q=P)).then_inc(rec_loaded, 16)
            store_table(0, AGG)
            sp.wait_ge(rec_free, 1)
            sp.dma_start(REC[:, 0:NT_S, :],
                         rec_src[0:NT_S * P, :].rearrange("(t q) w -> q t w", q=P)).then_inc(rec_loaded, 16)

            sp.wait_ge(slot_rows, 1)
            sp.dma_start(dst_d[1:1 + P * SQ].rearrange("(p j) -> p j", p=P), sc_score).then_inc(dst_stored, 16)
            sp.dma_start(dst_d[0:1].rearrange("(p j) -> p j", p=1), guard[:, :]).then_inc(dst_stored, 16)
            sp.dma_start(dst_d[1 + P * SQ:2 + P * SQ].rearrange("(p j) -> p j", p=1), guard[:, :]).then_inc(dst_stored, 16)
            lo_rows = lo_d.rearrange("(p c s q) -> s p c q", p=P, c=SCAN_C, s=2)
            for i in range(2):
                sp.wait_ge(slot_rows, 2 + i)
                sp.dma_start(lo_rows[i], scan_view(1 + i).bitcast(BF16)[:, 0:SQ].rearrange("p (c q) -> p c q", q=P)).then_inc(slot_stored, 16)
            sp.wait_ge(dst_stored, 16 * 3)
            sp.dma_start(sc_tot, dst_d[0:P * SQ].rearrange("(p j) -> p j", p=P)).then_inc(neigh_loaded, 16)
            sp.dma_start(sc_ex, dst_d[2:2 + P * SQ].rearrange("(p j) -> p j", p=P)).then_inc(neigh_loaded, 16)
            sp.wait_ge(slot_stored, 16 * 2)

            store_table(1, H)
            store_table(2, TA)
            store_table(3, H)
            for l in range(NL):
                store_table(4 + l, TA)
                first = l * (SG + 1)
                def lo_group(g, place):
                    sp.dma_start(lo_ring[place], lo_d[bass.ds(g * GT * 2 * P, GT * 2 * P)].partition_broadcast(P)).then_inc(lo_landed[place], 16)
                sp.wait_ge(parts_ready, l + 1)
                sp.wait_ge(table_written, 16 * (l + 6))
                for g in range(LR):
                    lo_group(g, g)
                with sp.Fori(0, SG // LR - 1) as i:
                    for u in range(LR):
                        sp.wait_ge(oht_ready, i * LR + (first + u + 3))
                        lo_group(i * LR + (LR + u), u)
                sp.wait_ge(oht_ready, first + SG - 1)
                lo_group(SG, 0)
            sp.wait_ge(final_rows, 1)
            sp.dma_start(out[0:(NB - 1) * P, :].rearrange("(b p) f -> p b f", p=P), X[:, 0:NB - 1, :]).then_inc(out_written, 16)
            sp.dma_start(out[(NB - 1) * P:N, :], X[0:TAIL, NB - 1, :]).then_inc(out_written, 16)
            sp.wait_ge(out_written, 32)

        @block.scalar
        def _(act):
            loads = [(w0[:], W0), (w_self[:], a["L1_gnn_W_self"].rearrange("l k d -> k l d")),
                     (w_neigh[:], a["L1_gnn_W_neigh"].rearrange("l k d -> k l d")),
                     (w_gat[:], a["L3_gnn_Ws"].rearrange("l k d -> k l d")),
                     (w_mid[:], a["L3_gnn_mid_ws"].rearrange("l k d -> k l d")),
                     (b0[:], a["L0_gnn_b"].partition_broadcast(P)),
                     (gamma[:], a["L2_gnn_gamma"].partition_broadcast(P)),
                     (beta[:], a["L2_gnn_beta"].partition_broadcast(P)),
                     (kern[:], a["L2_gnn_kernels"].rearrange("o d -> (o d)").partition_broadcast(P)),
                     (b1[:].rearrange("p l d -> p (l d)"), a["L1_gnn_bias"].rearrange("l d -> (l d)").partition_broadcast(P)),
                     (a_src[:].rearrange("p l d -> p (l d)"), a["L3_gnn_a_srcs"].rearrange("l d -> (l d)").partition_broadcast(P)),
                     (a_dst[:].rearrange("p l d -> p (l d)"), a["L3_gnn_a_dsts"].rearrange("l d -> (l d)").partition_broadcast(P)),
                     (b3[:].rearrange("p l d -> p (l d)"), a["L3_gnn_biases"].rearrange("l d -> (l d)").partition_broadcast(P))]
            for k, name in enumerate(("src", "dst", "edge_type_1000")):
                loads.append((firsts_i[:, k, :], a[name][0:3].partition_broadcast(P)))
            for dst, src in loads:
                act.dma_start(dst, src).then_inc(weights_loaded, 16)
            act.wait_ge(blank_ready, 1)
            for rec in (rec_low, rec_dst, rec_src):
                rows = rec[0:DUMP, :].rearrange("(p c t) w -> p c t w", p=P, t=BLANK_T)
                for c in range(BLANKS):
                    act.dma_start(rows[:, c], blank).then_inc(blanked, 16)

            act.preload_act_table(ACT.Copy)
            for k, (nt, _, _) in enumerate(SORTS):
                act.wait_ge(sort_ready, k + 1)
                b = sort_base[k] // 2
                words = F_C if k == 0 else RW
                with act.Fori(0, nt // (2 * ST)) as i:
                    for h in range(2):
                        act.wait_ge(scattered[h], i * (16 * ST) + 16 * ST * (b + 1))
                        nc.scalar.copy(rec_ring[:, h, :, 0:words], REC[:, bass.ds((i * 2 + h) * ST, ST), 0:words]).then_inc(rec_staged, 1)

            def sqrt_step(k, t):
                act.wait_ge(var_ready, k + 1)
                nc.scalar.activation(t, t, ACT.Sqrt).then_inc(std_ready, 1)

            def copy_turned(m):
                for j in range(DENSE[m] * NBT):
                    t = dense_t[m] + j
                    n = BATCHES[j // DENSE[m]][1] * P
                    act.wait_ge(turned, t + 1)
                    if t >= 2:
                        act.wait_ge(turned_used, t - 1)
                    nc.scalar.copy(xt_ring[:, t % 2, 0:n], ps[:, t % 2, 0:n]).then_inc(turned_copied, 1)

            def stage_group(k, i, u):
                g = pass_base[k] + u
                act.wait_ge(tiles_done, i * RR + (g + 1))
                nc.scalar.copy(idx_ring[:, g % RR, :],
                               idx_of[PASSES[k][0]][:, bass.ds(i * (RR * GT) + u * GT, GT)]).then_inc(idx_staged, 1)

            def stage_indices(k0, k1):
                for k in range(k0, k1):
                    act.wait_ge(pass_ready, k + 1)
                    each_group(act, k, lambda i, u: stage_group(k, i, u))

            def stage_rest(k):
                with act.Fori(0, (pass_base[k + 1] - pass_base[k]) // RR - 1) as i:
                    for u in range(RR):
                        stage_group(k, i, RR + u)

            sqrt_step(0, smallB[:])
            sqrt_step(1, rs_dst[:])
            sqrt_step(2, rs_src[:])
            act.wait_ge(slots_ready, 1)
            for u in range(RR):
                stage_group(0, 0, u)
            stage_rest(0)
            copy_turned(0)
            sqrt_step(3, smallB[:])
            stage_indices(1, 2)
            copy_turned(1)
            stage_indices(2, 3)
            copy_turned(2)
            for u in range(RR):
                stage_group(3, 0, u)
            act.wait_ge(gate_in, 1)
            nc.scalar.activation(flat(TA), flat(TA), ACT.Exp, scale=-1.0).then_inc(gate_out, 1)
            sqrt_step(4, smallB[:])
            sqrt_step(5, bn_row[:])
            stage_rest(3)
            stage_indices(4, 7)
            sqrt_step(6, smallB[:])
            for l in range(NL):
                copy_turned(m_rows(l))
                for u in range(RR):
                    stage_group(7 + l, 0, u)
                act.wait_ge(parts_ready, l + 1)
                with act.Fori(0, SG // 2) as i:
                    for h in range(2):
                        act.wait_ge(score_mm, i * 2 + (l * SG + h + 1))
                        nc.scalar.copy(hd_ring[:, h], hd_tiles[:, :, bass.ds(i * (2 * GT) + h * GT, GT)]).then_inc(hd_staged, 1)
                act.wait_ge(exp_in, l + 1)
                nc.scalar.activation(sc_ex, sc_ex, ACT.Exp).then_inc(exp_out, 1)
                stage_rest(7 + l)
                if 1 <= l <= MID:
                    copy_turned(m_mid(l))

        @block.gpsimd
        def _(pool):
            nc.gpsimd.iota(col_i[:], [[1, NT_A]], base=0, channel_multiplier=0).then_inc(iotas, 1)
            nc.gpsimd.iota(pid_i[:], [[0, 1]], base=0, channel_multiplier=1).then_inc(iotas, 1)

            group = pool.alloc_register("group")
            pool.reg_mov(group, 0)
            pool.wait_ge(blanked, 16 * 3 * BLANKS)
            for h in range(2):
                pool.dma_start(rec_low[SPARE + h * ST:SPARE + (h + 1) * ST, :], blank[0:ST, 0, :]).then_inc(scattered[h], 16 * ST)
            for k, (nt, _, rec) in enumerate(SORTS):
                g0 = sort_base[k]
                with pool.Fori(0, nt // (2 * ST)) as i:
                    for h in range(2):
                        pool.reg_add(group, group, 1)
                        pool.wait_ge(sort_ready, k + 1)
                        pool.wait_ge(pos_ready, group)
                        pool.wait_ge(rec_staged, group)
                        for j in range(ST):
                            pool.indirect_dma_start(
                                rec, bass.IndirectOffsetOnAxis(ap=pos_ring[:, h, j:j + 1], axis=0),
                                rec_ring[:, h, j, :], None).then_inc(scattered[h], 16)

            pool.reg_mov(group, 0)
            tables = 0
            for k, (kind, _, clears, _) in enumerate(PASSES):
                if kind == "dst":
                    tables += 1
                tab = table_r if kind.endswith("rel") else table

                def gather_group(i, u):
                    place = (pass_base[k] + u) % RR
                    pool.reg_add(group, group, 1)
                    pool.wait_ge(table_written, 16 * (tables + 1))
                    pool.wait_ge(idx_staged, group)
                    for j in range(GT):
                        pool.indirect_dma_start(
                            rows_in[place][:, j, :], None, tab,
                            bass.IndirectOffsetOnAxis(ap=idx_ring[:, place, j:j + 1], axis=0)).then_inc(landed[place], 16)
                each_group(pool, k, gather_group)

        @block.tensor
        def _(pe):
            pe.wait_ge(vcol_ready, 1)
            KE = NL * ED
            nc.tensor.transpose(ps[0:P, 7, 0:KE], base_col[0:KE, :], ident[0:KE, 0:KE]).then_inc(vproj_ready, 1)

            def dst_degrees(i):
                pe.wait_ge(dst_onehots, i + 1)
                for j in range(GT):
                    mm = nc.tensor.matmul(ps[:, 0, 0:6 * NB], oh_dlo[:, j, :], oh_dhi[:, j, :, :].rearrange("p l c -> p (l c)"),
                                          start=False, stop=False, skip_group_check=True)
                mm.then_inc(dst_multiplied, 1)

            def src_degrees(i):
                pe.wait_ge(src_onehots, i + 1)
                for j in range(GT):
                    mm = nc.tensor.matmul(ps[:, 1, 0:NB], oh_slo[:, j, :], oh_shi[:, j, :],
                                          start=False, stop=False, skip_group_check=True)
                mm.then_inc(src_multiplied, 1)

            nc.tensor.matmul(ps[:, 0, :], ones[:], zeros[:], start=True, stop=False, skip_group_check=True).then_inc(dst_multiplied, 1)
            nc.tensor.matmul(ps[:, 1, :], ones[:], zeros[:], start=True, stop=False, skip_group_check=True)

            pe.wait_ge(counts_ready, 1)
            nc.tensor.matmul(ps[:, 4, 0:NB], ones_f[:], cnt[:], start=True, stop=True).then_inc(counts_summed, 1)

            for k, (nt, bins, _) in enumerate(SORTS):
                g0 = sort_base[k]
                if k == 1:
                    src_degrees(EC // GT)
                    pe.wait_ge(counts_ready, 2)
                    nc.tensor.matmul(ps[:, 2, 0:1], before_f[:], col1[:], start=True, stop=True)
                    nc.tensor.matmul(ps[:, 3, 0:NB], ones_f[:], cnt[:], start=True, stop=True).then_inc(counts_summed, 1)
                    pe.wait_ge(counts_ready, 3)
                    nc.tensor.transpose(ps[:, 5, 0:P], base_col[:], ident[:]).then_inc(counts_summed, 1)
                    pe.wait_ge(ends_ready, 1)
                    for q, row in enumerate((tiles_end[:, 0, :], tiles_end[:, 1, :], smallB[:])):
                        mm = nc.tensor.transpose(ps[0:NB, 3, q * P:(q + 1) * P], row, ident[:])
                    mm.then_inc(blocks_found, 1)
                    pe.wait_ge(ends_ready, 2)
                    for q, banks in enumerate(((0, 1), (4, 7))):
                        for c, bank in enumerate(banks):
                            mm = nc.tensor.matmul(ps[0:1, bank, 0:NT_A // 2], ones[0:NB, 0:1],
                                                  past[:, q, c * (NT_A // 2):(c + 1) * (NT_A // 2)], start=True, stop=True)
                    mm.then_inc(blocks_found, 1)
                chain = ps[:, 6, :].rearrange("p (j c) -> p j c", c=P)[:, :, 0:bins]
                pe.wait_ge(sort_ready, k + 1)
                nc.tensor.matmul(chain, ident[:], base[:, k:k + 1, 0:bins].to_broadcast([P, ST, bins]),
                                 start=True, stop=False, skip_group_check=True)
                with pe.Fori(0, nt // (2 * ST)) as i:
                    for h in range(2):
                        oh = oh_ring[:, h, :, 0:bins]
                        pe.wait_ge(onehot_ready, i * 2 + (g0 + h + 1 + k))
                        for j in range(ST - 1):
                            nc.tensor.matmul(chain[:, j + 1:ST], ones[:], oh[:, j:j + 1].to_broadcast([P, ST - 1 - j, bins]),
                                             start=False, stop=False, skip_group_check=True)
                        nc.tensor.matmul(chain, before[:], oh, start=False, stop=False,
                                         skip_group_check=True).then_inc(prefix_ready, 1)
                        if k == 0:
                            (src_degrees, dst_degrees)[h](i)
                        pe.wait_ge(prefix_read, i * 2 + (g0 + h + 1))
                        for j in range(1, ST):
                            nc.tensor.matmul(chain[:, 0:j], ones[:], oh[:, j:j + 1].to_broadcast([P, j, bins]),
                                             start=False, stop=False, skip_group_check=True)
                        nc.tensor.matmul(chain, not_before[:], oh, start=False, stop=False, skip_group_check=True)

            def to_scan(k, t):
                pe.wait_ge(layout_src, k + 1)
                for c in range(SCAN_C):
                    mm = nc.tensor.transpose(psf[:, 2048 + c * P:2048 + (c + 1) * P], t[:].rearrange("q (p c) -> q c p", c=SCAN_C)[:, c, :], ident[:])
                mm.then_inc(layout_done, 1)

            def to_tiles(k, v):
                pe.wait_ge(layout_src, k + 1)
                for c in range(SCAN_C):
                    mm = nc.tensor.transpose(psf[:, 2048 + c * P:2048 + (c + 1) * P], v[:, c * P:(c + 1) * P], ident[:])
                mm.then_inc(layout_done, 1)

            def carries(k):
                pe.wait_ge(carry_in, 2 * k + 1)
                nc.tensor.transpose(ps[0:1, 6, 0:P], carry_col[:], ident[:]).then_inc(carry_t, 1)
                pe.wait_ge(carry_in, 2 * k + 2)
                nc.tensor.transpose(ps[:, 7, 0:1], row_b[:], ident[0:1, 0:1]).then_inc(carry_t, 1)

            def dense(m, sources, att=None):
                for q, (b, n) in enumerate(BATCHES):
                    pe.wait_ge(dense_src, m * NBT + q + 1)
                    for s, (rows, w) in enumerate(sources):
                        t = dense_t[m] + q * len(sources) + s
                        if t >= 2:
                            pe.wait_ge(turned_copied, t - 1)
                        for j in range(n):
                            mm = nc.tensor.transpose(ps[:, t % 2, j * P:(j + 1) * P], rows[:, b + j, :], ident[:])
                        mm.then_inc(turned, 1)
                    u = dense_b[m] + q
                    if u >= 2:
                        pe.wait_ge(dense_read, u - 1)
                    for s, (rows, w) in enumerate(sources):
                        t = dense_t[m] + q * len(sources) + s
                        pe.wait_ge(turned_copied, t + 1)
                    for j in range(n):
                        for s, (rows, w) in enumerate(sources):
                            t = dense_t[m] + q * len(sources) + s
                            mm = nc.tensor.matmul(ps[:, 2 + u % 2, j * D:(j + 1) * D], xt_ring[:, t % 2, j * P:(j + 1) * P], w,
                                                  start=(s == 0), stop=(s == len(sources) - 1))
                        if att is not None:
                            mm = nc.tensor.matmul(ps[:, 7, 2 * (b + j):2 * (b + j) + 2], xt_ring[:, t % 2, j * P:(j + 1) * P], att,
                                                  start=True, stop=True)
                    mm.then_inc(turned_used, len(sources))

            def aggregate(k):
                kind, _, clears, _ = PASSES[k]
                blk = blk_d if kind[:3] == "dst" else blk_s
                g0 = pass_base[k]
                if clears:
                    pe.wait_ge(pass_ready, k + 1)
                    for q in range(7):
                        nc.tensor.matmul(ps[:, q, :], ones[:], zeros[:], start=True, stop=False, skip_group_check=True)

                def multiply_group(i, u):
                    g = g0 + u
                    blocks = tile_blocks(pe, blk, i * (RR * GT // PACK) + u * GT // PACK)
                    pe.wait_ge(weights_ready, i * RR + (g + 1))
                    pe.wait_ge(landed[g % RR], i * (16 * GT) + 16 * GT * (g // RR + 1))
                    for j in range(GT):
                        if k >= 7:
                            nc.tensor.matmul(psf[:, bass.ds(blocks[j] + W_SUM, 1)], dw_ring[:, u % 2, j, :], ones_f[:, 0:1],
                                             start=False, stop=False, skip_group_check=True)
                        mm = nc.tensor.matmul(psf[:, bass.ds(blocks[j] * D, D)], dw_ring[:, u % 2, j, :], rows_in[g % RR][:, j, :],
                                              start=False, stop=False, skip_group_check=True)
                    mm.then_inc(tiles_done, 1)
                each_group(pe, k, multiply_group)

            def scores(l):
                pe.wait_ge(hd_in, 2 * l + 1)
                nc.tensor.transpose(ps[0:NB, 6, 0:P], smallB[:], ident[:]).then_inc(hd_out, 1)
                pe.wait_ge(hd_in, 2 * l + 2)
                for part in range(3):
                    for c in range(2):
                        mm = nc.tensor.matmul(ps[:, 2 * part + c, 0:NT_A // 2], hd_parts[:, part, :],
                                              tile_block[:, c * (NT_A // 2):(c + 1) * (NT_A // 2)], start=True, stop=True)
                mm.then_inc(hd_out, 1)
                pe.wait_ge(parts_ready, l + 1)
                with pe.Fori(0, SG // 2) as i:
                    for h in range(2):
                        pe.wait_ge(oht_ready, i * 2 + (l * (SG + 1) + h + 3))
                        pe.wait_ge(score_read, i * 2 + (l * SG + h + 1))
                        pe.wait_ge(hd_staged, i * 2 + (l * SG + h + 1))
                        pg = tiles_bank(h)
                        for j in range(GT):
                            for part in range(3):
                                nc.tensor.matmul(pg[:, j, 0:NB], oht_ring[:, h, j, 0, :],
                                                 hs_parts[:, part, :], start=(part == 0), stop=False)
                            for part in range(3):
                                mm = nc.tensor.matmul(pg[:, j, 0:NB], oht_ring[:, h, j, 1, :],
                                                      hd_ring[:, h, part, j:j + 1].to_broadcast([P, NB]),
                                                      start=False, stop=(part == 2))
                        mm.then_inc(score_mm, 1)

            pe.sem_inc(tiles_done, RR)
            pe.sem_inc(score_mm, 2)
            to_scan(0, t_alpha)
            pe.wait_ge(layout_read, 1)
            to_scan(1, t_srclo)
            pe.wait_ge(layout_read, 2)
            to_scan(2, t_lo)
            for k in range(2):
                pe.wait_ge(carry_in, k + 1)
                nc.tensor.transpose(ps[0:1, 6, 0:P], carry_col[:], ident[:]).then_inc(carry_t, 1)
            pe.wait_ge(weights_loaded, 16 * (1 + NL + 16))
            aggregate(0)
            dense(0, [(AGG, w0[:])])
            aggregate(1)
            dense(1, [(AGG, w_neigh[:, 0]), (H, w_self[:, 0])])
            aggregate(2)
            dense(2, [(AGG, w_neigh[:, 1]), (TA, w_self[:, 1])])
            for k, rows in enumerate((H, TB)):
                pe.wait_ge(bn_src, k + 1)
                for b in range(NB):
                    mm = nc.tensor.matmul(ps[:, 7, 0:D], ones_f[:], rows[:, b, :], start=(b == 0), stop=(b == NB - 1))
                mm.then_inc(bn_sum, 1)
            for k in range(3, 7):
                aggregate(k)
            lay, car = 3, 1
            for l in range(NL):
                src = {0: H}.get(l, AGG)
                dense(m_rows(l), [(src, w_gat[:, l])], w_att[:, l])
                scores(l)
                to_scan(lay, t_alpha)
                for c in range(2):
                    carries(car + c)
                car += 2
                to_tiles(lay + 1, sc_ex)
                lay += 2
                aggregate(7 + l)
                if 1 <= l <= MID:
                    dense(m_mid(l), [(AGG, w_mid[:, l - 1])])

        @block.vector
        def _(v):
            V = nc.vector
            def bc(t, shape):
                return t.to_broadcast(shape)

            V.memset(blank, 0.0)
            V.memset(zeros[:], 0.0)
            V.memset(ones[:], 1.0)
            V.memset(ones_f[:], 1.0)
            V.memset(guard[:], -2.0)
            V.memset(cnt[:], 0.0)
            V.memset(rec_ring[:], 0.0)
            V.memset(dw_ring[:], 0.0)
            V.memset(oh_shi_t[:], 0.0)
            v.drain()
            V.memset(blank[:, :, F_DST:F_DST + 1], -1.0).then_inc(blank_ready, 1)
            V.memset(recf, 0.0)
            v.drain()
            V.memset(REC[:, :, F_DST:F_DST + 1], -1.0)
            v.wait_ge(iotas, NCONST)
            V.tensor_copy(col_f[:], col_i[:])
            V.tensor_copy(pid_f[:], pid_i[:])
            v.drain()
            V.tensor_scalar(ident[:], col_f[:, 0:P], pid_f[:], None, ALU.is_equal)
            V.tensor_scalar(before_f[:], col_f[:, 0:P], pid_f[:], None, ALU.is_gt)
            V.tensor_scalar(before[:], col_f[:, 0:P], pid_f[:], None, ALU.is_gt)
            V.tensor_scalar(not_before[:], col_f[:, 0:P], pid_f[:], None, ALU.is_le)
            V.tensor_scalar(node_id[:], col_f[:, 0:NB], float(P), pid_f[:], ALU.mult, ALU.add)
            V.tensor_scalar(dump_f[:], pid_f[:], float(DUMP), None, ALU.add)
            v.drain()
            V.tensor_scalar(is_node[:], node_id[:], float(N), None, ALU.is_lt)
            V.tensor_copy(block_b[:], col_f[:, 0:NB])
            v.wait_ge(weights_loaded, 16 * (1 + NL + 16))
            V.tensor_tensor(aprod, wes, aedge, ALU.mult)
            v.drain()
            V.tensor_reduce(vcol[0:NL * ED, :], aprod, AX_X, ALU.add)
            v.drain()
            V.tensor_copy(base_col[0:NL * ED, :], bc(vcol[0:NL * ED, :], [NL * ED, P])).then_inc(vcol_ready, 1)
            v.wait_ge(vproj_ready, 1)
            V.tensor_copy(vproj[:], ps[:, 7, 0:NL * ED])
            v.wait_ge(edges_loaded, 64)
            for f, view in ((F_SRC, src_i), (F_DST, dst_i), (F_TYPE, type_i), (F_W, w_in)):
                V.tensor_copy(REC[0:EP, 0:EC, f], view)
            V.memset(REC[0:EP, 0:EC, F_VALID:F_VALID + 1], 1.0)
            for vals, lo, hi in ((dst_i, lo_dst, hi_dst), (src_i, lo_src, hi_src)):
                V.tensor_scalar(dig_i, vals, P - 1, None, ALU.bitwise_and)
                v.drain()
                V.tensor_copy(lo, dig_i)
                v.drain()
                V.tensor_scalar(dig_i, vals, 7, None, ALU.arith_shift_right)
                v.drain()
                V.tensor_copy(hi, dig_i)
                v.drain()
            loops = slice(EC, EC + NB)
            V.tensor_copy(REC[:, loops, F_SRC], node_id[:])
            V.tensor_copy(REC[:, loops, F_DST], node_id[:])
            v.drain().then_inc(src_onehots, 1)
            for b, n in BATCHES:
                V.tensor_tensor(src_eq[:, 0:n, :], bc(col_f[0:EP, b:b + n].unsqueeze(2), [EP, n, EC]),
                                bc(hi_src.unsqueeze(1), [EP, n, EC]), ALU.is_equal)
                v.drain()
                V.tensor_reduce(cnt[0:EP, b:b + n], src_eq[:, 0:n, :], AX_X, ALU.add)
                v.drain()

            def tiles_and_base(k, bank, b_i):
                V.tensor_scalar(smallA[:], ps[:, bank, 0:NB], float(P - 1), None, ALU.add)
                v.drain()
                V.tensor_copy(tiles_i[:], smallA[:])
                v.drain()
                V.tensor_scalar(tiles_i[:], tiles_i[:], 7, None, ALU.arith_shift_right)
                v.drain()
                V.tensor_copy(tiles_of[:], tiles_i[:])
                v.drain()
                V.tensor_tensor_scan(tiles_end[:, k, :], ones_f[:, 0:NB], tiles_of[:], 0.0, ALU.mult, ALU.add)
                v.drain()
                V.tensor_tensor(smallB[:], tiles_end[:, k, :], tiles_of[:], ALU.subtract)
                v.drain()
                V.tensor_scalar(base[:, b_i, 0:NB], smallB[:], float(P), None, ALU.mult)

            v.drain().then_inc(counts_ready, 1)
            v.wait_ge(counts_summed, 1)
            tiles_and_base(1, 4, 0)

            def sort_pass(k, beside=None, arrivals=(None,)):
                stretches = len(arrivals)
                nt, bins, _ = SORTS[k]
                turns = nt // (2 * ST) // stretches
                assert turns * stretches * 2 * ST == nt
                io = col_f[:, 0:bins].unsqueeze(1)

                def onehot(h, first):
                    return V.tensor_tensor(oh_ring[:, h, :, 0:bins], bc(io, [P, ST, bins]),
                                           bc(key[:, bass.ds(first, ST)].unsqueeze(2), [P, ST, bins]), ALU.is_equal)

                v.drain()
                onehot(0, 0).then_inc(onehot_ready, 1)
                v.drain().then_inc(sort_ready, 1)
                for stretch in range(stretches):
                    t0 = stretch * turns * 2 * ST
                    g0 = sort_base[k] + t0 // ST
                    if beside:
                        v.wait_ge(arrivals[stretch], 16)
                    with v.Fori(0, turns) as i:
                        for h in range(2):
                            tl = bass.ds(i * 2 * ST + (t0 + h * ST), ST)
                            prod = rank_prod[:, :, 0:bins]
                            v.wait_ge(prefix_ready, i * 2 + (g0 + h + 1))
                            V.tensor_tensor(prod, ps[:, 6, :].rearrange("p (j c) -> p j c", c=P)[:, :, 0:bins],
                                            oh_ring[:, h, :, 0:bins], ALU.mult).then_inc(prefix_read, 1)
                            onehot(1 - h, i * 2 * ST + (t0 + (h + 1) * ST)).then_inc(onehot_ready, 1)
                            V.tensor_scalar(inv[:, h], col_f[:, tl], float(P), dump_f[:], ALU.mult, ALU.add)
                            v.drain()
                            V.tensor_reduce(posf[:, h], prod, AX_X, ALU.add)
                            V.scalar_tensor_tensor(out=inv[:, h], in0=key[:, tl], scalar=0.0, in1=inv[:, h], op0=ALU.is_lt, op1=ALU.mult)
                            v.drain()
                            v.wait_ge(scattered[h], i * (16 * ST) + 16 * ST * (g0 // 2 + 1))
                            V.tensor_tensor(pos_ring[:, h, :], posf[:, h], inv[:, h], ALU.add).then_inc(pos_ready, 1)
                            if beside:
                                beside(stretch, i, h)
                v.wait_ge(prefix_ready, sort_base[k + 1])
                v.drain()

            iota_p = bc(col_f[0:EP, 0:P].unsqueeze(1), [EP, GT, P])
            iota_b = bc(col_f[0:EP, 0:NB].unsqueeze(1), [EP, GT, NB])

            def scores_and_degrees(stretch, i, h):
                c0 = stretch * EA_COLS
                tl = bass.ds(i * GT + c0, GT)
                turn = stretch * (EA_COLS // GT)
                if h == 0:
                    here = ea[stretch][:, bass.ds(i * GT, GT), :]
                    V.tensor_tensor(ea_prod, bc(here.unsqueeze(1), [EP, NL, GT, ED]),
                                    bc(vproj[0:EP].rearrange("p (l k) -> p l k", k=ED).unsqueeze(2), [EP, NL, GT, ED]), ALU.mult)
                    v.wait_ge(dst_multiplied, i + (turn + 1))
                    V.tensor_tensor(oh_dhi[:, :, 0, :], iota_b, bc(hi_dst[:, tl].unsqueeze(2), [EP, GT, NB]), ALU.is_equal)
                    V.tensor_tensor(oh_dlo, iota_p, bc(lo_dst[:, tl].unsqueeze(2), [EP, GT, P]), ALU.is_equal)
                    v.drain()
                    V.tensor_reduce(REC[0:EP, tl, F_C:F_C + NL].rearrange("p t l -> p l t"), ea_prod, AX_X, ALU.add)
                    v.drain()
                    V.tensor_tensor(oh_dhi[:, :, 1:6, :], bc(oh_dhi[:, :, 0:1, :], [EP, GT, NL, NB]),
                                    bc(REC[0:EP, tl, F_C:F_C + NL].unsqueeze(3), [EP, GT, NL, NB]), ALU.mult).then_inc(dst_onehots, 1)
                else:
                    v.wait_ge(src_multiplied, i + (turn + 1))
                    V.tensor_tensor(oh_slo, iota_p, bc(lo_src[:, tl].unsqueeze(2), [EP, GT, P]), ALU.is_equal)
                    V.tensor_tensor(oh_shi, iota_b, bc(hi_src[:, tl].unsqueeze(2), [EP, GT, NB]), ALU.is_equal).then_inc(src_onehots, 1)

            V.memset(key[:], -1.0)
            v.drain()
            V.tensor_copy(key[0:EP, 0:EC], hi_src)
            sort_pass(0, scores_and_degrees, attr_loaded)
            v.wait_ge(dst_multiplied, EC // GT + 1)
            v.wait_ge(src_multiplied, EC // GT + 1)
            V.memset(X[:, NB - 1, :], 0.0).then_inc(x_cleared, 1)
            V.tensor_copy(deg_dst[:], ps[:, 0, 0:NB])
            V.tensor_copy(deg_src[:], ps[:, 1, 0:NB])
            v.drain()
            V.tensor_scalar(rs_dst[:], deg_dst[:], 1.0, None, ALU.max)
            V.tensor_scalar(rs_src[:], deg_src[:], 1.0, None, ALU.max)
            V.tensor_tensor(cnt[:], deg_dst[:], is_node[:], ALU.add)
            v.drain()
            V.tensor_reduce(col1[:], cnt[:], AX_X, ALU.add)
            v.drain().then_inc(counts_ready, 1)
            V.reciprocal(rdeg[:], rs_dst[:])
            v.drain()
            for l in range(NL):
                V.tensor_tensor(REC[:, loops, F_C + l], ps[:, 0, (1 + l) * NB:(2 + l) * NB], rdeg[:], ALU.mult)
            v.wait_ge(counts_summed, 2)
            V.tensor_copy(base_col[:], bc(ps[:, 2, 0:1], [P, P])).then_inc(counts_ready, 1)
            tiles_and_base(0, 3, 2)
            v.drain().then_inc(ends_ready, 1)
            v.wait_ge(counts_summed, 3)
            V.tensor_copy(base[:, 1, :], ps[:, 5, 0:P])
            v.wait_ge(blocks_found, 1)
            for q in range(3):
                V.tensor_copy(ends_col[:, q:q + 1], ps[0:NB, 3, q * P:q * P + 1])
            v.drain()
            for q in range(2):
                V.tensor_scalar(past[:, q, :], col_f[0:NB, :], ends_col[:, q:q + 1], None, ALU.is_ge)
            v.drain().then_inc(ends_ready, 1)
            V.scalar_tensor_tensor(out=tile_block[:], in0=col_f[0:NB, :], scalar=ends_col[:, 2:3], in1=past[:, 0, :],
                                   op0=ALU.is_ge, op1=ALU.subtract)
            v.wait_ge(blocks_found, 2)
            for blk, banks in ((blk_d, (0, 1)), (blk_s, (4, 7))):
                for c, bank in enumerate(banks):
                    V.tensor_scalar(blk_row[:, c * (NT_A // 2):(c + 1) * (NT_A // 2)], ps[0:1, bank, 0:NT_A // 2],
                                    float(NB - 1), None, ALU.min)
                v.drain()
                tiles = blk_row.rearrange("p (t j) -> p t j", j=PACK)
                V.tensor_copy(blk_pack, tiles[:, :, PACK - 1])
                for j in reversed(range(PACK - 1)):
                    v.drain()
                    V.scalar_tensor_tensor(out=blk_pack, in0=blk_pack, scalar=32.0, in1=tiles[:, :, j], op0=ALU.mult, op1=ALU.add)
                v.drain()
                V.tensor_copy(blk[:], blk_pack)
            v.wait_ge(rel_loaded, 16)
            V.tensor_tensor(relr, relr, bc(kern[0:EP].unsqueeze(1), [EP, R // EP, D]), ALU.mult).then_inc(rel_rows, 1)
            V.memset(key[:], -1.0)
            v.drain()
            V.tensor_copy(key[0:EP, 0:EC], lo_dst)
            V.tensor_scalar(smallA[:], is_node[:], pid_f[:], None, ALU.mult)
            v.drain()
            V.tensor_tensor(smallA[:], smallA[:], is_node[:], ALU.add)
            v.drain()
            V.tensor_scalar(key[:, loops], smallA[:], -1.0, None, ALU.add)
            sort_pass(1)
            v.wait_ge(rec_loaded, 16)
            V.memset(key[:], -1.0)
            hi_i = t_alpha[:, 0:NT_HIGH].bitcast(I32)
            V.tensor_copy(hi_i, REC[:, 0:NT_HIGH, F_DST])
            v.drain()
            V.tensor_scalar(hi_i, hi_i, 7, None, ALU.arith_shift_right)
            v.drain()
            V.tensor_copy(key[:, 0:NT_HIGH], hi_i)
            sort_pass(2)

            def rows3(t, b=NB):
                return bc(t.unsqueeze(1), [P, b, D])

            def cols3(t):
                return bc(t.unsqueeze(2), [P, NB, D])

            def rsqrt_of(root, square, tmp):
                V.reciprocal(root, root)
                v.drain()
                V.tensor_tensor(tmp, root, root, ALU.mult)
                v.drain()
                V.tensor_tensor(tmp, tmp, square, ALU.mult)
                v.drain()
                V.tensor_scalar(tmp, tmp, -0.5, 1.5, ALU.mult, ALU.add)
                v.drain()
                V.tensor_tensor(root, root, tmp, ALU.mult)
                v.drain()

            def norm(k):
                v.drain()
                V.tensor_reduce(smallB[:], X[:], AX_X, ALU.add)
                v.drain()
                V.tensor_scalar(smallB[:], smallB[:], -1.0 / D, None, ALU.mult)
                v.drain()
                V.tensor_tensor(TA[:], X[:], cols3(smallB[:]), ALU.add)
                v.drain()
                V.tensor_tensor(TB[:], TA[:], TA[:], ALU.mult)
                v.drain()
                V.tensor_reduce(smallA[:], TB[:], AX_X, ALU.add)
                v.drain()
                V.tensor_scalar(smallA[:], smallA[:], 1.0 / D, EPS, ALU.mult, ALU.add)
                v.drain()
                V.tensor_copy(smallB[:], smallA[:]).then_inc(var_ready, 1)
                v.wait_ge(std_ready, k + 1)
                rsqrt_of(smallB[:], smallA[:], smallC[:])
                V.scalar_tensor_tensor(out=H[:], in0=TA[:], scalar=0.0, in1=cols3(smallB[:]), op0=ALU.max, op1=ALU.mult)
                v.drain()

            def weigh(k):
                kind, wt, _, _ = PASSES[k]
                lo = t_lo if kind[:3] == "dst" else s_lo
                w = wt_of[(kind[:3], wt)]
                g0 = pass_base[k]

                def weigh_group(i, u):
                    v.wait_ge(tiles_done, i * RR + (g0 + u + RR - 1))
                    for j in range(GT):
                        tl = bass.ds(i * (RR * GT) + (u * GT + j), 1)
                        last = V.tensor_scalar(dw_ring[:, u % 2, j, :], col_f[:, 0:P], lo[:, tl], w[:, tl],
                                               ALU.is_equal, ALU.mult)
                    last.then_inc(weights_ready, 1)
                each_group(v, k, weigh_group)

            def gather_sum(k0, k1, meanwhile=None):
                v.drain().then_inc(pass_ready, 1)
                for k in range(k0, k1):
                    if k > k0:
                        v.drain().then_inc(pass_ready, 1)
                    weigh(k)
                if meanwhile:
                    meanwhile()
                v.wait_ge(tiles_done, pass_base[k1] + RR)

            acc3 = acc.rearrange("p (b d) -> p b d", d=D)

            def each_product(m, f):
                for q, (b, n) in enumerate(BATCHES):
                    u = dense_b[m] + q
                    v.wait_ge(turned_used, dense_t[m] + (q + 1) * DENSE[m])
                    f(ps[:, 2 + u % 2, 0:n * D].rearrange("p (j d) -> p j d", d=D), slice(b, b + n), n)
                    v.drain().then_inc(dense_read, 1)

            v.wait_ge(x_loaded, 32)
            norm(0)
            v.sem_inc(var_ready, 2)
            v.wait_ge(std_ready, 3)
            V.tensor_scalar(smallA[:], deg_dst[:], 1.0, None, ALU.max)
            V.tensor_scalar(smallB[:], deg_src[:], 1.0, None, ALU.max)
            v.drain()
            rsqrt_of(rs_dst[:], smallA[:], smallC[:])
            rsqrt_of(rs_src[:], smallB[:], smallC[:])
            V.tensor_tensor(AGG[:], H[:], cols3(rs_src[:]), ALU.mult).then_inc(table_rows, 1)

            v.wait_ge(rec_loaded, 32)
            lo_i = flat(TB)[:, 0:NT_D].bitcast(I32)

            def low_digits(out_t, n, field, pad_field):
                V.tensor_copy(lo_i[:, 0:n], REC[:, 0:n, field])
                v.drain()
                V.tensor_scalar(lo_i[:, 0:n], lo_i[:, 0:n], P - 1, None, ALU.bitwise_and)
                V.tensor_scalar(t_alpha[:, 0:n], REC[:, 0:n, pad_field], 0.0, -float(2 * P), ALU.is_lt, ALU.mult)
                v.drain()
                V.tensor_tensor(out_t, lo_i[:, 0:n], t_alpha[:, 0:n], ALU.add)
                v.drain()

            V.tensor_copy(t_src[:], REC[:, :, F_SRC])
            v.drain().then_inc(slots_ready, 1)
            V.memset(t_lo[:], -1.0)
            V.memset(t_srclo[:], 0.0)
            v.drain()
            low_digits(t_lo[:, 0:NT_D], NT_D, F_DST, F_DST)
            low_digits(t_srclo[:, 0:NT_D], NT_D, F_SRC, F_SRC)
            V.tensor_copy(lo_i, REC[:, :, F_SRC])
            V.memset(t_hi[:, NT_D:NT_D + GT], 0.0)
            v.drain()
            V.tensor_scalar(lo_i, lo_i, 7, None, ALU.arith_shift_right)
            v.drain()
            V.tensor_copy(t_hi[:, 0:NT_D], lo_i)
            v.drain()
            V.tensor_copy(t_type[:], REC[:, :, F_TYPE])
            V.tensor_copy(t_w[:], REC[:, :, F_W])
            V.tensor_copy(t_valid[:], REC[:, :, F_VALID])
            v.drain()
            V.memset(t_alpha[:], -1.0)
            for l in range(NL):
                V.tensor_copy(t_c[:, l, :], REC[:, :, F_C + l])
            v.drain()
            V.tensor_copy(t_alpha[:, 0:NT_D], REC[:, :, F_DST])
            v.drain().then_inc(rec_free, 1)
            v.wait_ge(rec_loaded, 48)
            f_dst, f_type, f_lo, f_valid, f_neg = s_found
            V.tensor_scalar(f_dst.bitcast(U32), REC[:, 0:NT_S, F_DST], 0.0, None, ALU.max)
            V.tensor_copy(f_type.bitcast(U32), REC[:, 0:NT_S, F_TYPE])
            V.tensor_copy(f_valid, REC[:, 0:NT_S, F_VALID])
            V.tensor_scalar(f_neg, REC[:, 0:NT_S, F_VALID], -1.0, None, ALU.mult)
            V.tensor_copy(lo_i[:, 0:NT_S], REC[:, 0:NT_S, F_SRC])
            v.drain()
            V.tensor_scalar(lo_i[:, 0:NT_S], lo_i[:, 0:NT_S], P - 1, None, ALU.bitwise_and)
            v.drain()
            V.tensor_copy(f_lo, lo_i[:, 0:NT_S])
            v.drain().then_inc(layout_src, 1)

            psv = psf[:, 2048:2048 + SQ]
            v.wait_ge(layout_done, 1)
            V.tensor_copy(sc_score, psv).then_inc(slot_rows, 1)
            v.drain().then_inc(layout_read, 1)
            for k in range(2):
                v.drain().then_inc(layout_src, 1)
                v.wait_ge(layout_done, 2 + k)
                V.tensor_copy(scan_view(1 + k).bitcast(BF16)[:, 0:SQ], psv).then_inc(slot_rows, 1)
                v.drain().then_inc(layout_read, 1)
            v.wait_ge(neigh_loaded, 32)
            V.tensor_tensor(sc_keepf, sc_score, sc_tot, ALU.is_equal)
            V.tensor_tensor(sc_keepb, sc_score, sc_ex, ALU.is_equal)
            v.drain()
            V.tensor_scalar(sc_neg, sc_keepf, BIG, -BIG, ALU.mult, ALU.add)
            V.tensor_scalar(sc_end, sc_keepb, -1.0, 1.0, ALU.mult, ALU.add)
            for k, keep in enumerate((sc_keepf, sc_keepb)):
                v.drain()
                V.tensor_reduce(carry_col[:], keep, AX_X, ALU.min)
                v.drain().then_inc(carry_in, 1)
                v.wait_ge(carry_t, k + 1)
                V.tensor_copy(keep_rows[:, 1 + k, :], ps[0:1, 6, 0:P])
            v.drain()
            V.tensor_scalar(keep_rows[:, 0, :], keep_rows[:, 1, :], BIG, -BIG, ALU.mult, ALU.add)
            v.wait_ge(slot_stored, 32)
            for found, kept in zip(s_found, s_kept):
                V.tensor_copy(kept.bitcast(I32), found.bitcast(I32))


            gather_sum(0, 1)
            V.tensor_tensor(AGG[:], acc3, cols3(rs_dst[:]), ALU.mult)
            v.drain().then_inc(dense_src, NBT)

            def gcn(prod, blocks, n):
                V.tensor_tensor(TA[:, blocks, :], prod, rows3(b0[:], n), ALU.add)
                v.drain()
                V.scalar_tensor_tensor(out=X[:, blocks, :], in0=TA[:, blocks, :], scalar=0.0, in1=X[:, blocks, :],
                                       op0=ALU.max, op1=ALU.add)
            each_product(0, gcn)

            norm(3)
            v.drain().then_inc(table_rows, 1)
            gather_sum(1, 2)
            V.tensor_tensor(AGG[:], acc3, cols3(rdeg[:]), ALU.mult)
            v.drain().then_inc(dense_src, NBT)

            def sage_relu(prod, blocks, n):
                V.tensor_tensor(TA[:, blocks, :], prod, rows3(b1[:, 0], n), ALU.add)
                v.drain()
                V.tensor_scalar(TA[:, blocks, :], TA[:, blocks, :], 0.0, None, ALU.max)
            each_product(1, sage_relu)
            v.drain().then_inc(table_rows, 1)
            gather_sum(2, 3)
            V.tensor_tensor(AGG[:], acc3, cols3(rdeg[:]), ALU.mult)
            v.drain().then_inc(dense_src, NBT)

            def sage_gate(prod, blocks, n):
                V.tensor_tensor(TB[:, blocks, :], prod, rows3(b1[:, 1], n), ALU.add)
            each_product(2, sage_gate)
            V.tensor_scalar(TA[:], TB[:], -80.0, None, ALU.max).then_inc(gate_in, 1)
            v.wait_ge(gate_out, 1)
            V.tensor_scalar(TA[:], TA[:], 1.0, None, ALU.add)
            v.drain()
            V.reciprocal(TA[:], TA[:])
            v.drain()
            V.tensor_tensor(X[:], X[:], TA[:], ALU.add)

            norm(4)
            V.tensor_tensor(H[:], H[:], cols3(is_node[:]), ALU.mult)
            v.drain().then_inc(bn_src, 1)
            v.wait_ge(bn_sum, 1)
            V.tensor_scalar(bn_row[:], ps[:, 7, 0:D], -1.0 / N, None, ALU.mult)
            v.drain()
            V.tensor_tensor(TA[:], H[:], rows3(bn_row[:]), ALU.add)
            v.drain()
            V.tensor_tensor(TA[:], TA[:], cols3(is_node[:]), ALU.mult)
            v.drain()
            V.tensor_tensor(TB[:], TA[:], TA[:], ALU.mult)
            v.drain().then_inc(bn_src, 1)
            v.wait_ge(bn_sum, 2)
            V.tensor_scalar(b0[:], ps[:, 7, 0:D], 1.0 / N, EPS, ALU.mult, ALU.add)
            v.drain()
            V.tensor_copy(bn_row[:], b0[:]).then_inc(var_ready, 1)
            v.wait_ge(std_ready, 6)
            rsqrt_of(bn_row[:], b0[:], bn_tmp[:])
            V.tensor_tensor(bn_row[:], bn_row[:], gamma[:], ALU.mult)
            v.drain()
            V.tensor_tensor(TA[:], TA[:], rows3(bn_row[:]), ALU.mult)
            v.drain()
            V.tensor_tensor(TA[:], TA[:], rows3(beta[:]), ALU.add)
            v.drain()
            V.tensor_tensor(H[:], TA[:], rows3(kern[:]), ALU.mult)
            v.drain().then_inc(table_rows, 1)
            V.tensor_copy(firsts[:], firsts_i[:])
            V.memset(cnt[:], 1.0)
            for k in range(3):
                v.drain()
                V.tensor_tensor(col1[:], firsts[:, k, 0:1], firsts[:, k, 2:3], ALU.not_equal)
                for e in (0, 2):
                    v.drain()
                    V.tensor_scalar(smallA[:], node_id[:], firsts[:, k, e:e + 1], col1[:], ALU.is_equal, ALU.mult)
                    v.drain()
                    V.tensor_tensor(cnt[:], cnt[:], smallA[:], ALU.add)
            v.drain()
            V.reciprocal(cnt[:], cnt[:])

            def gat_weights():
                for l in range(NL):
                    for q, av in enumerate((a_src, a_dst)):
                        V.tensor_tensor(bn_row[:], w_gat[:, l], av[:, l], ALU.mult)
                        v.drain()
                        V.tensor_reduce(w_att[:, l, q:q + 1], bn_row[:], AX_X, ALU.add)
                        v.drain()
                V.tensor_scalar(b3_mix[:], b3[:], 1.0 - ALPHA, None, ALU.mult)
                for l in range(1, MID + 1):
                    keep = math.log(THETA / l + 1.0)
                    V.tensor_scalar(bn_row[:], ident[:], 1.0 - keep, None, ALU.mult)
                    v.drain()
                    V.scalar_tensor_tensor(out=w_mid[:, l - 1], in0=w_mid[:, l - 1], scalar=keep, in1=bn_row[:],
                                           op0=ALU.mult, op1=ALU.add)
                    v.drain()
            gather_sum(3, 7, gat_weights)
            V.tensor_tensor(AGG[:], acc3, H[:], ALU.add)
            v.drain()
            V.tensor_tensor(AGG[:], AGG[:], cols3(cnt[:]), ALU.mult)
            v.drain()
            V.tensor_tensor(X[:], X[:], AGG[:], ALU.add)

            norm(6)
            v.drain().then_inc(dense_src, NBT)
            v.sem_inc(score_read, 2)
            v.sem_inc(oht_ready, 2)

            def take_rows(prod, blocks, n):
                V.tensor_copy(TA[:, blocks, :], prod)

            def split(parts, hs):
                V.tensor_copy(parts[:, 0, :], hs)
                for q in (0, 1):
                    v.drain()
                    V.tensor_tensor(hs, hs, parts[:, q, :], ALU.subtract)
                    v.drain()
                    V.tensor_copy(parts[:, q + 1, :], hs)

            def carry(k, keep_row, col, op0, op1, start, back):
                V.tensor_copy(carry_col[:], col)
                v.drain().then_inc(carry_in, 1)
                v.wait_ge(carry_t, 2 * k + 1)
                V.tensor_copy(row_a[:], ps[0:1, 6, 0:P])
                V.memset(carry_row[:], start)
                v.drain()
                r = slice(None, None, -1) if back else slice(None)
                V.tensor_tensor_scan(carry_row[:, 1:P + 1][:, r], keep_row[:, r], row_a[:, r], start, op0, op1)
                v.drain()
                V.tensor_copy(row_b[:], carry_row[:, 2:P + 2] if back else carry_row[:, 0:P])
                v.drain().then_inc(carry_in, 1)
                v.wait_ge(carry_t, 2 * k + 2)
                V.tensor_copy(carry_col[:], ps[:, 7, 0:1])
                v.drain()

            def segment_total(k, data, op0, op1, d0, keep_row, start):
                V.tensor_tensor_scan(sc_fwd, d0, data, start, op0, op1)
                v.drain()
                carry(k, keep_row, sc_fwd[:, SQ - 1:SQ], op0, op1, start, False)
                V.tensor_tensor_scan(sc_fwd, d0, data, carry_col[:], op0, op1)
                v.drain()
                V.tensor_tensor(sc_ends, sc_fwd, sc_end, ALU.mult)
                v.drain()
                V.tensor_tensor_scan(sc_tot[:, ::-1], sc_keepb[:, ::-1], sc_ends[:, ::-1], 0.0, ALU.mult, ALU.add)
                v.drain()
                carry(k + 1, keep_rows[:, 2, :], sc_tot[:, 0:1], ALU.mult, ALU.add, 0.0, True)
                V.tensor_tensor_scan(sc_tot[:, ::-1], sc_keepb[:, ::-1], sc_ends[:, ::-1], carry_col[:], ALU.mult, ALU.add)
                v.drain()

            lay, car = 3, 1
            for l in range(NL):
                each_product(m_rows(l), take_rows)
                v.sem_inc(table_rows, 1)
                att = ps[:, 7, 0:2 * NB].rearrange("p (b s) -> p b s", s=2)
                V.tensor_copy(smallB[:], att[:, :, 1])
                V.tensor_copy(smallA[:], att[:, :, 0])
                v.drain().then_inc(hd_in, 1)
                v.wait_ge(hd_out, 2 * l + 1)
                V.tensor_copy(hd_turned[:], ps[0:NB, 6, 0:P])
                v.drain()
                split(hd_parts, hd_turned[:])
                v.drain().then_inc(hd_in, 1)
                split(hs_parts, smallA[:])
                v.wait_ge(hd_out, 2 * l + 2)
                for part in range(3):
                    V.tensor_copy(hd_tiles[:, part, :].rearrange("p (c t) -> p c t", c=2),
                                  ps[:, 2 * part:2 * part + 2, 0:NT_A // 2])
                v.drain().then_inc(parts_ready, 1)
                n0 = l * SG

                def turn(u, i):
                    place = u % LR
                    before_l = l * (SG // LR + (place == 0))
                    v.wait_ge(lo_landed[place], i * (16 * UN // LR) + 16 * (before_l + u // LR + 1))
                    return V.tensor_scalar(oht_flat[:, u % 2], lo_ring[place], pid_f[:], None, ALU.is_equal)

                def source_blocks(h, first):
                    V.tensor_tensor(oh_hi[:, h], bc(block_b[:].unsqueeze(1), [P, GT, NB]),
                                    bc(t_hi[:, bass.ds(first, GT)].unsqueeze(2), [P, GT, NB]), ALU.is_equal)

                v.wait_ge(score_mm, n0 + 1)
                turn(0, 0).then_inc(oht_ready, 1)
                source_blocks(0, 0)
                v.drain()
                with v.Fori(0, SG // UN) as i:
                    for u in range(UN):
                        h = u % 2
                        v.wait_ge(score_mm, i * UN + (n0 + u + 2))
                        turn(u + 1, i).then_inc(oht_ready, 1)
                        source_blocks(1 - h, i * (UN * GT) + (u + 1) * GT)
                        v.wait_ge(score_mm, i * UN + (n0 + u + 3))
                        V.tensor_tensor(pr_hi[:, h], tiles_bank(h)[:, :, 0:NB], oh_hi[:, h],
                                        ALU.mult).then_inc(score_read, 1)
                        v.drain()
                        V.tensor_reduce(t_alpha[:, bass.ds(i * (UN * GT) + u * GT, GT)], pr_hi[:, h], AX_X, ALU.add)
                v.drain()
                V.memset(t_alpha[:, NT_D:NT_A], 0.0)
                V.tensor_tensor(t_alpha[:, 0:NT_D], t_alpha[:, 0:NT_D], t_c[:, l, :], ALU.add)
                v.drain()
                V.scalar_tensor_tensor(out=t_alpha[:], in0=t_alpha[:], scalar=ATT_SLOPE, in1=t_alpha[:], op0=ALU.mult, op1=ALU.max)
                v.drain().then_inc(layout_src, 1)
                v.wait_ge(layout_done, lay + 1)
                V.tensor_copy(sc_score, psv)
                v.drain()
                segment_total(car, sc_score, ALU.add, ALU.max, sc_neg, keep_rows[:, 0, :], -BIG)
                V.tensor_tensor(sc_ex, sc_score, sc_tot, ALU.subtract).then_inc(exp_in, 1)
                v.wait_ge(exp_out, l + 1)
                v.drain().then_inc(layout_src, 1)
                v.wait_ge(layout_done, lay + 2)
                V.tensor_copy(t_alpha[:].rearrange("q (p c) -> q c p", c=SCAN_C), psv.rearrange("q (c p) -> q c p", c=SCAN_C))
                lay, car = lay + 2, car + 2

                def mix_in():
                    V.scalar_tensor_tensor(out=TB[:], in0=X0[:], scalar=ALPHA, in1=rows3(b3_mix[:, l]), op0=ALU.mult, op1=ALU.add)
                mixed = 1 <= l <= MID
                gather_sum(7 + l, 8 + l, mix_in if mixed else None)
                V.tensor_scalar(smallA[:], psf[:, W_SUM:W_SUM + NB], 0.5, None, ALU.max)
                v.drain()
                V.reciprocal(smallA[:], smallA[:])
                v.drain()
                if mixed:
                    V.tensor_scalar(smallA[:], smallA[:], 1.0 - ALPHA, None, ALU.mult)
                    v.drain()

                V.tensor_tensor(AGG[:], acc3, cols3(smallA[:]), ALU.mult)
                v.drain()
                if l <= MID:
                    for b, n in BATCHES:
                        V.tensor_tensor(AGG[:, b:b + n, :], AGG[:, b:b + n, :],
                                        TB[:, b:b + n, :] if mixed else rows3(b3[:, l], n), ALU.add)
                        v.drain().then_inc(dense_src, 1)
                if l == 0:
                    V.tensor_copy(X0[:], AGG[:])
                elif l <= MID:
                    def mid(prod, blocks, n):
                        V.tensor_scalar(TA[:, blocks, :], prod, OUT_SLOPE, None, ALU.mult)
                        v.drain()
                        V.tensor_tensor(AGG[:, blocks, :], prod, TA[:, blocks, :], ALU.max)
                    each_product(m_mid(l), mid)
                    v.sem_inc(dense_src, NBT)
                else:
                    V.tensor_tensor(AGG[:], AGG[:], rows3(b3[:, l]), ALU.add)
                    v.drain()
                    V.tensor_tensor(X[:], X[:], AGG[:], ALU.add)
            v.drain().then_inc(final_rows, 1)


_INS = ["x", "src", "dst", "edge_attr_16", "edge_type_1000", "edge_weight", "L0_gnn_W", "L0_gnn_b", "L1_gnn_W_self",
        "L1_gnn_W_neigh", "L1_gnn_bias", "L2_gnn_r", "L2_gnn_gamma", "L2_gnn_beta", "L2_gnn_kernels", "L3_gnn_Ws",
        "L3_gnn_Wes", "L3_gnn_a_srcs", "L3_gnn_a_dsts", "L3_gnn_a_edges", "L3_gnn_biases", "L3_gnn_mid_ws"]


def kernel(**inputs):
    import concourse.bacc as _bacc
    from concourse.bass_utils import run_bass_kernel_spmd as _run

    nc = _bacc.Bacc("TRN2", target_bir_lowering=False, num_devices=1)
    arrays, args = {}, {}
    for name in _INS:
        arr = np.ascontiguousarray(inputs[name])
        arrays[f"in_{name}"] = arr
        args[name] = nc.dram_tensor(f"in_{name}", arr.shape, mybir.dt.from_np(arr.dtype), kind="ExternalInput").ap()
    out = nc.dram_tensor("out_x", inputs["x"].shape, F32, kind="ExternalOutput").ap()
    build(nc, args, out)
    r = _run(nc, [arrays], core_ids=[0])
    return r.results[0]["out_x"]
```
